# Optimizing a Trainium2 kernel written in Bass

```python
import numpy as np
import jax
import jax.numpy as jnp

def _softmax(x, axis=-1):
    return jax.nn.softmax(x, axis=axis)

def _gelu(x):
    return jax.nn.gelu(x, approximate=True)

def _silu(x):
    return jax.nn.silu(x)

def _sigmoid(x):
    return jax.nn.sigmoid(x)

def _layernorm(x, axis=-1, eps=1e-05):
    m = jnp.mean(x, axis=axis, keepdims=True)
    v = jnp.var(x, axis=axis, keepdims=True)
    return (x - m) / jnp.sqrt(v + eps)

def _scatter_add(tgt, idx, src, axis=0):
    return tgt.at[idx].add(src)

def _segment_sum(src, seg, n):
    return jax.ops.segment_sum(src, seg, n)
kernel_name = 'mk_cond_resid_d4_seqx_r4_8ca259'

def setup_inputs(seed: int=0):
    np.random.seed(seed)
    _w = jnp.asarray

    def _rec_inputs():
        import jax
        import jax.numpy as jnp
        _rk = jax.random.key(seed)
        x = -0.000125 + 0.9999 * jax.random.normal(jax.random.fold_in(_rk, 1), (64, 64, 512), jnp.float32)
        _lenS = 64 - jax.random.randint(jax.random.fold_in(_rk, 7), (64,), 0, max(1, 64 // 4) + 1, jnp.int32)
        _lenS2 = 64 - jax.random.randint(jax.random.fold_in(_rk, 8), (64,), 0, max(1, 64 // 4) + 1, jnp.int32)
        itok_B_0_3 = jax.random.randint(jax.random.fold_in(_rk, 11), (64,), 0, 4, jnp.int32)
        itok_B_0_6 = jax.random.randint(jax.random.fold_in(_rk, 12), (64,), 0, 7, jnp.int32)
        itok_B_0_7 = jax.random.randint(jax.random.fold_in(_rk, 13), (64,), 0, 8, jnp.int32)
        itok_B_1_198 = jax.random.randint(jax.random.fold_in(_rk, 14), (64,), 1, 199, jnp.int32)
        return (x, itok_B_0_3, itok_B_0_6, itok_B_0_7, itok_B_1_198)
    x, itok_B_0_3, itok_B_0_6, itok_B_0_7, itok_B_1_198 = _rec_inputs()

    def _L0_cond_setup():
        import jax, jax.numpy as jnp
        import numpy as np
        B, S, D_IN, D_OUT, R, E = (8, 512, 512, 512, 16, 4)
        key = jax.random.key(seed)
        ks = jax.random.split(key, 7)
        x = jax.random.normal(ks[0], (B, S, D_IN), dtype=jnp.float32)
        W_base = jax.random.normal(ks[1], (D_OUT, D_IN), dtype=jnp.float32) * 0.02
        Wt = jax.random.normal(ks[2], (D_IN, D_IN), dtype=jnp.float32) * 0.02
        A = jax.random.normal(ks[3], (E, R, D_IN), dtype=jnp.float32) * 0.02
        B_w = jax.random.normal(ks[4], (E, D_OUT, R), dtype=jnp.float32) * 0.02
        Wp = jax.random.normal(ks[5], (D_OUT, D_OUT), dtype=jnp.float32) * 0.02
        scaling = jnp.ones((E,), dtype=jnp.float32)
        adapter_idx = jax.random.randint(ks[6], (B,), 0, E)
        return {'x': x, 'W_base': W_base, 'Wt': Wt, 'A': A, 'B_w': B_w, 'Wp': Wp, 'scaling': scaling, 'adapter_idx': adapter_idx}
    _L0_cond_all = _L0_cond_setup()
    _L0_cond_in = {k: v for k, v in _L0_cond_all.items() if k in ('W_base', 'Wt', 'A', 'B_w', 'Wp', 'scaling')}
    del _L0_cond_all

    def _L1_cond_setup():
        import jax, jax.numpy as jnp
        import numpy as np
        B, T, D_IN, D_OUT = (16, 512, 512, 512)
        N_ADAPTERS, RANK = (8, 16)
        key = jax.random.key(seed)
        k_x, k_w, k_a, k_b, k_s, k_idx = jax.random.split(key, 6)
        x = jax.random.normal(k_x, (B, T, D_IN), dtype=jnp.float32)
        W = jax.random.normal(k_w, (D_OUT, D_IN), dtype=jnp.float32) * (1.0 / np.sqrt(D_IN))
        A = jax.random.normal(k_a, (N_ADAPTERS, RANK, D_IN), dtype=jnp.float32) * 0.02
        Bm = jax.random.normal(k_b, (N_ADAPTERS, D_OUT, RANK), dtype=jnp.float32) * 0.02
        scalings = jnp.ones((N_ADAPTERS,), dtype=jnp.float32)
        adapter_idx = jax.random.randint(k_idx, (B,), 0, N_ADAPTERS, dtype=jnp.int32)
        return {'x': x, 'W': W, 'A': A, 'Bm': Bm, 'scalings': scalings, 'adapter_idx': adapter_idx}
    _L1_cond_all = _L1_cond_setup()
    _L1_cond_in = {k: v for k, v in _L1_cond_all.items() if k in ('W', 'A', 'Bm', 'scalings')}
    del _L1_cond_all

    def _L2_cond_setup():
        import jax, jax.numpy as jnp
        import numpy as np
        B, C, D, T, N_SUBJECTS = (128, 64, 64, 512, 8)
        key = jax.random.key(seed)
        kx, ks, kw = jax.random.split(key, 3)
        x = jax.random.normal(kx, (B, C, T), dtype=jnp.float32)
        subjects = jax.random.randint(ks, (B,), 0, N_SUBJECTS, dtype=jnp.int64)
        weights = jax.random.normal(kw, (N_SUBJECTS, C, D), dtype=jnp.float32) * (1.0 / C ** 0.5)
        return {'x': x, 'subjects': subjects, 'weights': weights}
    _L2_cond_all = _L2_cond_setup()
    _L2_cond_in = {k: v for k, v in _L2_cond_all.items() if k in ('weights',)}
    del _L2_cond_all

    def _L3_cond_setup():
        import jax, jax.numpy as jnp
        import numpy as np
        B, C, T = (128, 64, 512)
        S, D = (200, 64)
        key = jax.random.key(seed)
        k1, k2, k3 = jax.random.split(key, 3)
        x = jax.random.normal(k1, (B, C, T), dtype=jnp.float32)
        conditions = jax.random.randint(k2, (B,), 0, S, dtype=jnp.int64)
        weights = jax.random.normal(k3, (S, C, D), dtype=jnp.float32) / jnp.sqrt(jnp.float32(C))
        return {'x': x, 'conditions': conditions, 'weights': weights}
    _L3_cond_all = _L3_cond_setup()
    _L3_cond_in = {k: v for k, v in _L3_cond_all.items() if k in ('weights',)}
    del _L3_cond_all
    return {'x': x, 'itok_B_0_3': itok_B_0_3, 'itok_B_0_6': itok_B_0_6, 'itok_B_0_7': itok_B_0_7, 'itok_B_1_198': itok_B_1_198, 'L0_cond_W_base': _L0_cond_in['W_base'], 'L0_cond_Wt': _L0_cond_in['Wt'], 'L0_cond_A': _L0_cond_in['A'], 'L0_cond_B_w': _L0_cond_in['B_w'], 'L0_cond_Wp': _L0_cond_in['Wp'], 'L0_cond_scaling': _L0_cond_in['scaling'], 'L1_cond_W': _L1_cond_in['W'], 'L1_cond_A': _L1_cond_in['A'], 'L1_cond_Bm': _L1_cond_in['Bm'], 'L1_cond_scalings': _L1_cond_in['scalings'], 'L2_cond_weights': _L2_cond_in['weights'], 'L3_cond_weights': _L3_cond_in['weights']}

def reference(x, itok_B_0_3, itok_B_0_6, itok_B_0_7, itok_B_1_198, L0_cond_W_base, L0_cond_Wt, L0_cond_A, L0_cond_B_w, L0_cond_Wp, L0_cond_scaling, L1_cond_W, L1_cond_A, L1_cond_Bm, L1_cond_scalings, L2_cond_weights, L3_cond_weights):
    import jax
    import jax.numpy as jnp

    def _L0_cond_ref(x, W_base, Wt, A, B_w, Wp, scaling, adapter_idx):
        import jax, jax.numpy as jnp
        import numpy as np
        B, S, D_IN, D_OUT, R, E = (8, 512, 512, 512, 16, 4)
        base = jnp.einsum('bsi,oi->bso', x, W_base)
        h = jnp.einsum('bsi,ji->bsj', x, Wt)
        Ab = A[adapter_idx]
        Bb = B_w[adapter_idx]
        sc = scaling[adapter_idx]
        z = jnp.einsum('bsj,brj->bsr', h, Ab)
        l = jnp.einsum('bsr,bor->bso', z, Bb)
        lora_out = jnp.einsum('bso,po->bsp', l, Wp) * sc[:, None, None]
        return base + lora_out

    def _L1_cond_ref(x, W, A, Bm, scalings, adapter_idx):
        import jax, jax.numpy as jnp
        import numpy as np
        B, T, D_IN, D_OUT = (16, 512, 512, 512)
        N_ADAPTERS, RANK = (8, 16)
        H = jnp.einsum('btd,od->bto', x, W)
        A_b = A[adapter_idx]
        B_b = Bm[adapter_idx]
        s_b = scalings[adapter_idx]
        xa = jnp.einsum('btd,brd->btr', x, A_b)
        delta = jnp.einsum('btr,bor->bto', xa, B_b)
        delta = jax.lax.stop_gradient(delta * s_b[:, None, None])
        return H + delta

    def _L2_cond_ref(x, subjects, weights):
        import jax, jax.numpy as jnp
        import numpy as np
        B, C, D, T, N_SUBJECTS = (128, 64, 64, 512, 8)
        w = weights[subjects]
        out = jnp.einsum('bct,bcd->bdt', x, w)
        return out

    def _L3_cond_ref(x, conditions, weights):
        import jax, jax.numpy as jnp
        import numpy as np
        B, C, T = (128, 64, 512)
        S, D = (200, 64)
        w = weights[conditions]
        return jnp.einsum('bct,bcd->bdt', x, w)
    x = x + _L0_cond_ref(x, L0_cond_W_base, L0_cond_Wt, L0_cond_A, L0_cond_B_w, L0_cond_Wp, L0_cond_scaling, itok_B_0_3)
    x = x + _L1_cond_ref(x, L1_cond_W, L1_cond_A, L1_cond_Bm, L1_cond_scalings, itok_B_0_6)
    x = x + _L2_cond_ref(x, itok_B_0_7, L2_cond_weights)
    x = x + _L3_cond_ref(x, itok_B_1_198, L3_cond_weights)
    return x

_drawn_inputs = setup_inputs


def setup_inputs(seed=0):
    import zlib

    import numpy as np

    out = dict(_drawn_inputs(seed))
    spreads = {'L0_cond_scaling': (1.0, 0.6), 'L1_cond_scalings': (1.0, 0.6)}
    factors = {'L0_cond_Wt': 8.0,
     'L0_cond_A': 8.0,
     'L0_cond_B_w': 8.0,
     'L0_cond_Wp': 8.0,
     'L0_cond_W_base': 5.857}
    for name, (base, spread) in spreads.items():
        noise = np.random.default_rng([zlib.crc32(name.encode()), seed]).standard_normal(out[name].shape)
        drawn = base * np.exp(spread * noise) if base else spread * noise
        out[name] = jnp.asarray(drawn.astype(out[name].dtype))
    for name, factor in factors.items():
        out[name] = (out[name] * factor).astype(out[name].dtype)
    return out
```

```python
from contextlib import ExitStack

import concourse.bass as bass
from concourse import mybir

ALU = mybir.AluOpType
ACT = mybir.ActivationFunctionType
F32 = mybir.dt.float32
F32R = mybir.dt.float32r
I32 = mybir.dt.int32

PART = 128
BATCH = 64
SEQ = 64
D = 512
RANK = 16
E0 = 4
E1 = 8
E2 = 8
E3 = 200

KC = D // PART
PAIRS = BATCH * SEQ // PART
QUAD = 4
QUADS = PAIRS // QUAD
R0 = E0 * RANK
R1 = E1 * RANK
T0_ROWS = 2 * E1 * R0
T_ROWS = T0_ROWS + 2 * R1


def wait(eng, sem, value):
    if not isinstance(value, int) or value > 0:
        eng.wait_ge(sem, value)


def build(nc, x, e0_ids, e1_ids, e2_ids, e3_ids, w_base, w_t, a0, b0, w_p, s0, w1, a1, b1, s1, w2, w3, out):
    ctx = ExitStack()
    with ctx:
        def sb(name, shape, dt=F32):
            return ctx.enter_context(nc.sbuf_tensor(name, shape, dt))

        def sem(name):
            return ctx.enter_context(nc.semaphore(name))

        v_table = nc.dram_tensor("v_table", [T_ROWS, D], F32, kind="Internal").ap()

        ident = sb("ident", [PART, PART])
        ident2 = sb("ident2", [PART, SEQ])
        owner = sb("owner", [PART, E1])
        ids = sb("ids", [PART, 4, BATCH], I32)


        wb_sb = sb("wb_sb", [PART, KC, D])
        wt_sb = sb("wt_sb", [PART, KC, D])
        wp_sb = sb("wp_sb", [PART, KC, D])
        w1_sb = sb("w1_sb", [PART, KC, D])
        a0_sb = sb("a0_sb", [R0, D])
        a1_sb = sb("a1_sb", [PART, D])
        b0_sb = sb("b0_sb", [PART, E0, KC, RANK])
        b1_sb = sb("b1_sb", [PART, E1, KC, RANK])
        s0_sb = sb("s0_sb", [PART, E0])
        s1_sb = sb("s1_sb", [PART, E1])
        w2_sb = sb("w2_sb", [PART, E2 // 2, SEQ])

        b0_by = sb("b0_by", [PART, KC, E0, RANK])
        b1_by = sb("b1_by", [PART, KC, E1, RANK])
        g1 = sb("g1", [PART, KC, D])
        wpT = sb("wpT", [PART, KC, D])
        a0T = sb("a0T", [PART, KC, R0])
        a1T = sb("a1T", [PART, KC, R1])
        v0T = sb("v0T", [PART, KC, 2, R0])
        v1 = sb("v1", [PART, D])
        v1_parts = sb("v1_parts", [PART, 2, D], F32R)
        cross = sb("cross", [PART, E1, R0])
        v0g1 = sb("v0g1", [PART, D])
        t0_sum = sb("t0_sum", [PART, 2, D])
        t0_parts = sb("t0_parts", [PART, 2, 2, D], F32R)
        gh = sb("gh", [PART, KC, D], F32R)
        gl = sb("gl", [PART, KC, D], F32R)
        u_tab = sb("u_tab", [PART, 2, KC, E0 + E1, RANK], F32R)
        w2T = sb("w2T", [PART, E2, SEQ])
        w3_all = sb("w3_all", [PART, PAIRS, SEQ])
        ph = sb("ph", [PART, PAIRS, PART], F32R)
        pl = sb("pl", [PART, PAIRS, PART], F32R)

        w2_diag = [sb(f"w2_diag{u}", [PART, PART]) for u in range(QUAD)]
        x_raw = sb("x_raw", [PART, QUAD, D])
        xh = [sb(f"xh{n}", [PART, D], F32R) for n in range(2)]
        xl = [sb(f"xl{n}", [PART, D], F32R) for n in range(2)]
        yh = [sb(f"yh{n}", [PART, KC, PART], F32R) for n in range(2)]
        yl = [sb(f"yl{n}", [PART, KC, PART], F32R) for n in range(2)]
        u_sel = [sb(f"u_sel{n}", [PART, 2, KC, PART], F32R) for n in range(2)]
        zh = [sb(f"zh{n}", [PART, PART], F32R) for n in range(2)]
        zl = [sb(f"zl{n}", [PART, PART], F32R) for n in range(2)]
        v_sel = [sb(f"v_sel{u}", [PART, D], F32R) for u in range(QUAD)]
        o_sb = sb("o_sb", [PART, QUAD, D])

        bank = [ctx.enter_context(nc.psum_tensor(f"bank{n}", [PART, D], F32)) for n in range(8)]
        y_ps, z_ps, o_ps, p_ps = bank[0:2], bank[2:4], bank[4:6], bank[6]

        ones_set = sem("ones_set")
        ident_set = sem("ident_set")
        ident2_set = sem("ident2_set")
        zero_set = sem("zero_set")
        ids_in = sem("ids_in")
        a1_in, w1_in, wb_in = sem("a1_in"), sem("w1_in"), sem("wb_in")
        a0_in, wt_in, wp_in = sem("a0_in"), sem("wt_in"), sem("wp_in")
        b0_in, b1_in, w2_in = sem("b0_in"), sem("b1_in"), sem("w2_in")
        w3_in = [sem(f"w3_in{n}") for n in range(2 * QUAD)]
        wb_plus = sem("wb_plus")
        b_scaled = sem("b_scaled")
        w3_plus = sem("w3_plus")
        setup_ps = sem("setup_ps")
        setup_act = sem("setup_act")
        setup_dve = sem("setup_dve")
        v1_out = sem("v1_out")
        t0_out = [sem(f"t0_out{n}") for n in range(2)]
        w2_placed = sem("w2_placed")
        p_done, ph_set, pl_set = sem("p_done"), sem("ph_set"), sem("pl_set")
        x_in = [sem(f"x_in{h}") for h in range(2)]
        xh_set, xl_set = sem("xh_set"), sem("xl_set")
        y_done, yh_set, yl_set = sem("y_done"), sem("yh_set"), sem("yl_set")
        u_placed = sem("u_placed")
        z_done, zh_set, zl_set = sem("z_done"), sem("zh_set"), sem("zl_set")
        v_in = [sem(f"v_in{u}") for u in range(QUAD)]
        o_done, o_set = sem("o_done"), sem("o_set")
        o_out = [sem(f"o_out{h}") for h in range(2)]

        x_rows = x.rearrange("(n b) s d -> n (b s) d", b=2).rearrange("n p d -> p n d")
        out_rows = out.rearrange("(n b) s d -> n (b s) d", b=2).rearrange("n p d -> p n d")
        w3_flat = w3.rearrange("e c d -> (e c) d")

        ORDER = ["a1T", "w2T", "g1_0", "g1_1", "g1_2", "g1_3", "a0T",
                 "wpT_0", "wpT_1", "wpT_2", "wpT_3", "v1",
                 "g01_0", "g01_1", "g01_2", "g01_3", "gu1", "u0", "v0T",
                 "cross", "v0g1", "t0_0", "t0_1", "t0_2", "t0_3"]
        ACT_STEPS = ["a1T", "g1_0", "g1_1", "g1_2", "g1_3", "wpT_0", "wpT_1", "wpT_2", "wpT_3",
                     "v1", "v1_high", "g01_0", "g01_1", "g01_2", "g01_3", "gu1", "u0", "v0g1"]
        DVE_STEPS = ["w2T_0", "w2T", "g1_0", "g1_1", "g1_2", "g1_3", "a0T", "v1_low",
                     "g01_0", "g01_1", "g01_2", "g01_3", "gu1", "u0", "v0T", "cross",
                     "t0_0", "t0_0_high", "t0_0_low", "t0_1", "t0_1_high", "t0_1_low",
                     "t0_2", "t0_2_high", "t0_2_low", "t0_3", "t0_3_high", "t0_3_low"]
        ACT_DONE = {name: n + 1 for n, name in enumerate(ACT_STEPS)}
        DVE_DONE = {name: n + 1 for n, name in enumerate(DVE_STEPS)}
        place = {name: n for n, name in enumerate(ORDER)}

        def bank_of(name):
            return bank[place[name] % 8]

        block = ctx.enter_context(nc.Block())

        @block.sync
        def _(sp):
            sp.dma_start(a1_sb[:, :], a1.rearrange("f r d -> (f r) d")).then_inc(a1_in, 16)
            sp.dma_start(w1_sb[:, :, :], w1.rearrange("(c p) d -> p c d", p=PART)).then_inc(w1_in, 16)
            sp.dma_start(wb_sb[:, :, :], w_base.rearrange("(c p) d -> p c d", p=PART)).then_inc(wb_in, 16)
            sp.dma_start(wp_sb[:, :, :], w_p.rearrange("(c p) d -> p c d", p=PART)).then_inc(wp_in, 16)
            sp.dma_start(wt_sb[:, :, :], w_t.rearrange("(c p) d -> p c d", p=PART)).then_inc(wt_in, 16)

            def load(i, h):
                wait(sp, xl_set, QUAD * (i - 1) + 2 * h + 2)
                sp.dma_start(x_raw[:, 2 * h:2 * h + 2, :],
                             x_rows[:, bass.ds(QUAD * i + 2 * h, 2), :]).then_inc(x_in[h], 16)

            def store(i, h):
                sp.wait_ge(o_set, QUAD * i + 2 * h + 2)
                sp.dma_start(out_rows[:, bass.ds(QUAD * i + 2 * h, 2), :],
                             o_sb[:, 2 * h:2 * h + 2, :]).then_inc(o_out[h], 16)

            for h in range(2):
                load(0, h)

            sp.wait_ge(ids_in, 64)

            def index(row, n, count):
                return sp.value_load(ids[0:1, row, bass.ds(n, 1)], min_val=0, max_val=count - 1)

            def fetch_w3(i):
                for n in range(2 * QUAD):
                    wait(sp, w3_in[n], 16 * i)
                    e = index(3, 2 * QUAD * i + n, E3)
                    sp.dma_start(w3_all[SEQ * (n % 2):SEQ * (n % 2) + SEQ, bass.ds(QUAD * i + n // 2, 1), :]
                                 .rearrange("p a d -> p (a d)"),
                                 w3_flat[bass.ds(e * SEQ, SEQ), :]).then_inc(w3_in[n], 16)

            def fetch_v(i, u):
                wait(sp, o_done, QUAD * (i - 1) + u + 1)
                for b in range(2):
                    e = index(0, 2 * (QUAD * i + u) + b, E0)
                    f = index(1, 2 * (QUAD * i + u) + b, E1)
                    for part, row in ((0, f * (2 * R0) + e * (2 * RANK)), (1, f * (2 * RANK) + T0_ROWS)):
                        to = 64 * b + 32 * part
                        sp.dma_start(v_sel[u][to:to + 32, :].bitcast(F32),
                                     v_table[bass.ds(row, 2 * RANK), :]).then_inc(v_in[u], 16)

            fetch_w3(0)
            fetch_w3(1)
            sp.wait_ge(setup_dve, DVE_DONE["v1_low"])
            sp.dma_start(v_table[T0_ROWS:, :].rearrange("(p h) d -> p (h d)", h=2),
                         v1_parts[:, :, :].rearrange("p h d -> p (h d)").bitcast(F32)).then_inc(v1_out, 16)
            t0_rows = v_table[0:T0_ROWS, :].rearrange("(n p h) d -> n p (h d)", h=2, p=PART)
            for n in range(E1 // 2):
                sp.wait_ge(setup_dve, DVE_DONE[f"t0_{n}_low"])
                sp.dma_start(t0_rows[n], t0_parts[:, n % 2, :, :].rearrange("p h d -> p (h d)").bitcast(F32)
                             ).then_inc(t0_out[n % 2], 16)
            sp.wait_ge(v1_out, 16)
            for n in range(2):
                sp.wait_ge(t0_out[n], 32)
            for u in range(QUAD):
                fetch_v(0, u)

            def turn(i, last=False):
                for h in range(2):
                    if not last:
                        load(i + 1, h)
                        if not (isinstance(i, int) and i == QUADS - 2) and h == 0:
                            fetch_w3(i + 2)
                    store(i, h)
                    if not last:
                        for u in range(2 * h, 2 * h + 2):
                            fetch_v(i + 1, u)

            turn(0)
            with sp.Fori(1, QUADS - 2) as i:
                turn(i)
            turn(QUADS - 2)
            turn(QUADS - 1, last=True)
            for h in range(2):
                sp.wait_ge(o_out[h], 16 * QUADS)

        @block.gpsimd
        def _(pool):
            nc.gpsimd.memset(ident[:, :], 0.0).then_inc(ones_set, 1)
            nc.gpsimd.memset(owner[:, :], 1.0).then_inc(ones_set, 1)
            pool.wait_ge(ones_set, 2)
            nc.gpsimd.affine_select(out=ident[:, :], in_=ident[:, :], compare_op=ALU.not_equal, fill=1.0,
                                    base=0, pattern=[[-1, PART]], channel_multiplier=1).then_inc(ident_set, 1)
            nc.gpsimd.affine_select(out=owner[:, :], in_=owner[:, :], compare_op=ALU.is_ge, fill=0.0,
                                    base=0, pattern=[[-RANK, E1]], channel_multiplier=1).then_inc(ones_set, 1)
            pool.wait_ge(ones_set, 3)
            nc.gpsimd.affine_select(out=owner[:, :], in_=owner[:, :], compare_op=ALU.is_ge, fill=0.0,
                                    base=RANK - 1, pattern=[[RANK, E1]], channel_multiplier=-1).then_inc(ident_set, 1)
            for t in w2_diag:
                nc.gpsimd.memset(t[:, :], 0.0).then_inc(zero_set, 1)
            for t in zh + zl:
                nc.gpsimd.memset(t[:, :].bitcast(F32), 0.0).then_inc(zero_set, 1)
            nc.gpsimd.memset(ph[:, :, :].bitcast(F32), 0.0).then_inc(zero_set, 1)
            nc.gpsimd.memset(pl[:, :, :].bitcast(F32), 0.0).then_inc(zero_set, 1)

            pool.wait_ge(ids_in, 64)

            def place_u(i, u):
                for b in range(2):
                    for part, (row, first, count) in enumerate(((0, 0, E0), (1, E0, E1))):
                        e = pool.value_load(ids[0:1, row, bass.ds(2 * (QUAD * i + u) + b, 1)],
                                            min_val=0, max_val=count - 1)
                        col = 64 * b + 32 * part
                        dst = u_sel[u % 2][:, :, :, col:col + 32].rearrange("p h k (r t) -> p (h k) r t", t=2)
                        src = u_tab[:, :, :, bass.ds(e + first, 1), :].rearrange("p h k a r -> p (h k) (a r)").unsqueeze(3)
                        nc.gpsimd.tensor_copy(dst, src.to_broadcast([PART, 2 * KC, RANK, 2])).then_inc(u_placed, 1)

            pool.wait_ge(setup_dve, DVE_DONE["u0"])
            for u in range(2):
                place_u(0, u)
            def turn(i, last=False):
                for u in range(QUAD):
                    if not (last and u >= 2):
                        pool.wait_ge(z_done, QUAD * i + u + 1)
                        place_u(i + (u + 2) // QUAD, (u + 2) % QUAD)

            turn(0)
            with pool.Fori(1, QUADS - 1) as i:
                turn(i)
            turn(QUADS - 1, last=True)

        @block.scalar
        def _(act):
            for n, t in enumerate((e0_ids, e1_ids, e2_ids, e3_ids)):
                act.dma_start(ids[:, n, :], t.partition_broadcast(PART)).then_inc(ids_in, 16)
            act.dma_start(w2_sb[:, :, :], w2.rearrange("(n g) c d -> (g c) n d", g=2)).then_inc(w2_in, 16)
            act.dma_start(a0_sb[:, :], a0.rearrange("e r d -> (e r) d")).then_inc(a0_in, 16)
            act.dma_start(b0_sb[:, :, :, :], b0.rearrange("e (p s) r -> p e s r", s=KC)).then_inc(b0_in, 16)
            act.dma_start(b1_sb[:, :, :, :], b1.rearrange("e (p s) r -> p e s r", s=KC)).then_inc(b1_in, 16)
            act.dma_start(s0_sb[:, :], s0.partition_broadcast(PART)).then_inc(b0_in, 16)
            act.dma_start(s1_sb[:, :], s1.partition_broadcast(PART)).then_inc(b1_in, 16)

            def read(name, dst, src):
                act.wait_ge(setup_ps, place[name] + 1)
                nc.scalar.activation(dst, src, ACT.Copy).then_inc(setup_act, 1)

            read("a1T", a1T[:, :, :].rearrange("p k r -> p (k r)"), bank_of("a1T")[:, :])
            for k in range(KC):
                read(f"g1_{k}", g1[:, k, :], bank_of(f"g1_{k}")[:, :])
            for k in range(KC):
                read(f"wpT_{k}", wpT[:, k, :], bank_of(f"wpT_{k}")[:, :])
            read("v1", v1[:, :].rearrange("p (n s) -> p s n", s=KC),
                 bank_of("v1")[:, :].rearrange("p (s n) -> p s n", s=KC))
            act.wait_ge(setup_act, ACT_DONE["v1"])
            nc.scalar.activation(v1_parts[:, 0, :], v1[:, :], ACT.Copy).then_inc(setup_act, 1)
            for k in range(KC):
                read(f"g01_{k}", gh[:, k, :], bank_of(f"g01_{k}")[:, :])
            read("gu1", u_tab[:, 0, :, E0:, :].rearrange("p k e r -> p k (e r)"),
                 bank_of("gu1")[:, :].rearrange("p (k r) -> p k r", k=KC))
            read("u0", u_tab[:, 0, :, 0:E0, :].rearrange("p k e r -> p k (e r)"),
                 bank_of("u0")[:, 0:KC * R0].rearrange("p (k r) -> p k r", k=KC))
            read("v0g1", v0g1[:, :], bank_of("v0g1")[:, :])

            def split_x(i, u):
                i, u = i + u // QUAD, u % QUAD
                act.wait_ge(x_in[u // 2], 16 * (i + 1))
                wait(act, y_done, QUAD * i + u - 1)
                nc.scalar.activation(xh[u % 2][:, :], x_raw[:, u, :], ACT.Copy).then_inc(xh_set, 1)

            def high_y(i, u):
                i, u = i + u // QUAD, u % QUAD
                act.wait_ge(y_done, QUAD * i + u + 1)
                wait(act, o_done, QUAD * i + u - 1)
                nc.scalar.activation(yh[u % 2][:, :, :].rearrange("p k t -> p (k t)"), y_ps[u % 2][:, :],
                                     ACT.Copy).then_inc(yh_set, 1)

            def high_p(i):
                act.wait_ge(p_done, i + 1)
                for b in range(2):
                    rows = slice(SEQ * b, SEQ * b + SEQ)
                    nc.scalar.activation(ph[rows, bass.ds(QUAD * i, QUAD), SEQ * b:SEQ * b + SEQ],
                                         p_ps[rows, 0:QUAD * SEQ].rearrange("p (n d) -> p n d", d=SEQ),
                                         ACT.Copy).then_inc(ph_set, 1)

            def copy_out(i, u):
                act.wait_ge(o_done, QUAD * i + u + 1)
                wait(act, o_out[u // 2], 16 * i)
                nc.scalar.activation(o_sb[:, u, :], o_ps[u % 2][:, :], ACT.Copy).then_inc(o_set, 1)

            def step(i, u, last):
                high_y_due = not (last and u == QUAD - 1)
                if high_y_due:
                    high_y(i, u + 1)
                act.wait_ge(z_done, QUAD * i + u + 1)
                wait(act, o_done, QUAD * i + u - 1)
                for b in range(2):
                    rows, toks = slice(SEQ * b, SEQ * b + SEQ), slice(SEQ * b, SEQ * b + SEQ)
                    nc.scalar.activation(zh[u % 2][rows, toks], z_ps[u % 2][rows, toks], ACT.Copy).then_inc(zh_set, 1)
                if not (last and u >= QUAD - 2):
                    split_x(i, u + 2)
                if u == 1 and not last:
                    high_p(i + 1)
                copy_out(i, u)

            act.wait_ge(zero_set, 10)
            high_p(0)
            split_x(0, 0)
            split_x(0, 1)
            high_y(0, 0)
            for u in range(QUAD):
                step(0, u, False)
            with act.Fori(1, QUADS - 1) as i:
                for u in range(QUAD):
                    step(i, u, False)
            for u in range(QUAD):
                step(QUADS - 1, u, True)


        @block.vector
        def _(dve):
            dve.wait_ge(ident_set, 2)
            for b in range(2):
                half = slice(SEQ * b, SEQ * b + SEQ)
                nc.vector.tensor_copy(ident2[half, :], ident[half, half]).then_inc(ident2_set, 1)
            dve.wait_ge(wb_in, 16)
            for k in range(KC):
                blk = wb_sb[:, k, PART * k:PART * k + PART]
                nc.vector.tensor_tensor(blk, blk, ident[:, :], ALU.add).then_inc(wb_plus, 1)

            def read(name, dst, src, in1, op):
                dve.wait_ge(setup_ps, place[name] + 1)
                nc.vector.tensor_tensor(dst, src, in1, op).then_inc(setup_dve, 1)

            w2_bank = bank_of("w2T")[0:SEQ, :].rearrange("p (g c) -> p g c", c=SEQ)
            eye = ident[0:SEQ, 0:SEQ].unsqueeze(1).to_broadcast([SEQ, E2, SEQ])
            for b in range(2):
                read("w2T", w2T[SEQ * b:SEQ * b + SEQ, :, :], w2_bank, eye, ALU.add)
            for k in range(KC):
                dve.wait_ge(setup_act, ACT_DONE[f"g1_{k}"])
                blk = slice(PART * k, PART * k + PART)
                read(f"g1_{k}", g1[:, k, blk], bank_of(f"g1_{k}")[:, blk], ident[:, :], ALU.add)
            dve.wait_ge(setup_ps, place["a0T"] + 1)
            nc.vector.tensor_copy(a0T[:, :, :].rearrange("p k r -> p (k r)"),
                                  bank_of("a0T")[:, 0:KC * R0]).then_inc(setup_dve, 1)
            for (b_in, b_sb, b_by, s_sb, n) in ((b0_in, b0_sb, b0_by, s0_sb, E0), (b1_in, b1_sb, b1_by, s1_sb, E1)):
                dve.wait_ge(b_in, 32)
                nc.vector.tensor_tensor(b_by[:, :, :, :].rearrange("p s e r -> p e s r"), b_sb[:, :, :, :],
                                        s_sb[:, :].unsqueeze(2).unsqueeze(3).to_broadcast([PART, n, KC, RANK]),
                                        ALU.mult).then_inc(b_scaled, 1)
            dve.wait_ge(setup_act, ACT_DONE["v1"] + 1)
            nc.vector.tensor_tensor(v1_parts[:, 1, :], v1[:, :], v1_parts[:, 0, :].bitcast(F32),
                                    ALU.subtract).then_inc(setup_dve, 1)
            for k in range(KC):
                dve.wait_ge(setup_act, ACT_DONE[f"g01_{k}"])
                read(f"g01_{k}", gl[:, k, :], bank_of(f"g01_{k}")[:, :], gh[:, k, :].bitcast(F32), ALU.subtract)
            dve.wait_ge(setup_act, ACT_DONE["gu1"])
            read("gu1", u_tab[:, 1, :, E0:, :].rearrange("p k e r -> p k (e r)"),
                 bank_of("gu1")[:, :].rearrange("p (k r) -> p k r", k=KC),
                 u_tab[:, 0, :, E0:, :].rearrange("p k e r -> p k (e r)").bitcast(F32), ALU.subtract)
            dve.wait_ge(setup_act, ACT_DONE["u0"])
            read("u0", u_tab[:, 1, :, 0:E0, :].rearrange("p k e r -> p k (e r)"),
                 bank_of("u0")[:, 0:KC * R0].rearrange("p (k r) -> p k r", k=KC),
                 u_tab[:, 0, :, 0:E0, :].rearrange("p k e r -> p k (e r)").bitcast(F32), ALU.subtract)
            dve.wait_ge(setup_ps, place["v0T"] + 1)
            nc.vector.tensor_copy(v0T[:, :, :, :],
                                  bank_of("v0T")[:, 0:KC * R0].rearrange("p (k r) -> p k r", k=KC).unsqueeze(2)
                                  .to_broadcast([PART, KC, 2, R0])).then_inc(setup_dve, 1)
            read("cross", cross[:, :, :], bank_of("cross")[:, 0:R0].unsqueeze(1).to_broadcast([PART, E1, R0]),
                 owner[:, :].unsqueeze(2).to_broadcast([PART, E1, R0]), ALU.mult)
            dve.wait_ge(setup_act, ACT_DONE["v0g1"])
            for n in range(4):
                wait(dve, t0_out[n % 2], 16 * (n // 2))
                read(f"t0_{n}", t0_sum[:, n % 2, :], bank_of(f"t0_{n}")[:, :], v0g1[:, :], ALU.add)
                dve.wait_ge(setup_dve, DVE_DONE[f"t0_{n}"])
                nc.vector.tensor_copy(t0_parts[:, n % 2, 0, :], t0_sum[:, n % 2, :]).then_inc(setup_dve, 1)
                dve.wait_ge(setup_dve, DVE_DONE[f"t0_{n}"] + 1)
                nc.vector.tensor_tensor(t0_parts[:, n % 2, 1, :], t0_sum[:, n % 2, :],
                                        t0_parts[:, n % 2, 0, :].bitcast(F32), ALU.subtract).then_inc(setup_dve, 1)

            def split_x(i, u):
                i, u = i + u // QUAD, u % QUAD
                dve.wait_ge(xh_set, QUAD * i + u + 1)
                wait(dve, y_done, QUAD * i + u - 1)
                nc.vector.tensor_tensor(xl[u % 2][:, :], x_raw[:, u, :], xh[u % 2][:, :].bitcast(F32),
                                        ALU.subtract).then_inc(xl_set, 1)

            def low_y(i, u):
                i, u = i + u // QUAD, u % QUAD
                dve.wait_ge(yh_set, QUAD * i + u + 1)
                wait(dve, o_done, QUAD * i + u - 1)
                nc.vector.tensor_tensor(yl[u % 2][:, :, :].rearrange("p k t -> p (k t)"), y_ps[u % 2][:, :],
                                        yh[u % 2][:, :, :].rearrange("p k t -> p (k t)").bitcast(F32),
                                        ALU.subtract).then_inc(yl_set, 1)

            def low_p(i):
                dve.wait_ge(ph_set, 2 * (i + 1))
                for b in range(2):
                    rows = slice(SEQ * b, SEQ * b + SEQ)
                    blk = slice(SEQ * b, SEQ * b + SEQ)
                    nc.vector.tensor_tensor(pl[rows, bass.ds(QUAD * i, QUAD), blk],
                                            p_ps[rows, 0:QUAD * SEQ].rearrange("p (n d) -> p n d", d=SEQ),
                                            ph[rows, bass.ds(QUAD * i, QUAD), blk].bitcast(F32),
                                            ALU.subtract).then_inc(pl_set, 1)

            def add_w3(i):
                for n in range(2 * QUAD):
                    dve.wait_ge(w3_in[n], 16 * (i + 1))
                w = w3_all[:, bass.ds(QUAD * i, QUAD), :]
                nc.vector.tensor_tensor(w, w, ident2[:, :].unsqueeze(1).to_broadcast([PART, QUAD, SEQ]),
                                        ALU.add).then_inc(w3_plus, 1)

            def place_w2(i):
                wait(dve, p_done, i)
                for u in range(QUAD):
                    for b in range(2):
                        g = dve.value_load(ids[0:1, 2, bass.ds(2 * (QUAD * i + u) + b, 1)],
                                           min_val=0, max_val=E2 - 1)
                        rows = slice(SEQ * b, SEQ * b + SEQ)
                        nc.vector.tensor_copy(w2_diag[u][rows, rows],
                                              w2T[rows, bass.ds(g, 1), :].rearrange("p a c -> p (a c)")
                                              ).then_inc(w2_placed, 1)

            def step(i, u, last):
                if u == 0 and not last:
                    add_w3(i + 1)
                    place_w2(i + 1)
                if not (last and u == QUAD - 1):
                    low_y(i, u + 1)
                dve.wait_ge(zh_set, 2 * (QUAD * i + u + 1))
                wait(dve, o_done, QUAD * i + u - 1)
                for b in range(2):
                    rows, toks = slice(SEQ * b, SEQ * b + SEQ), slice(SEQ * b, SEQ * b + SEQ)
                    nc.vector.tensor_tensor(zl[u % 2][rows, toks], z_ps[u % 2][rows, toks],
                                            zh[u % 2][rows, toks].bitcast(F32), ALU.subtract).then_inc(zl_set, 1)
                if not (last and u >= QUAD - 2):
                    split_x(i, u + 2)
                if u == 1 and not last:
                    low_p(i + 1)

            dve.wait_ge(ident2_set, 2)
            add_w3(0)
            dve.wait_ge(zero_set, 10)
            place_w2(0)
            low_p(0)
            split_x(0, 0)
            split_x(0, 1)
            low_y(0, 0)
            for u in range(QUAD):
                step(0, u, False)
            with dve.Fori(1, QUADS - 1) as i:
                for u in range(QUAD):
                    step(i, u, False)
            for u in range(QUAD):
                step(QUADS - 1, u, True)

        @block.tensor
        def _(pe):
            def free_bank(name):
                n = place[name] - 8
                if n >= 0:
                    before = ORDER[n]
                    if before in ACT_DONE:
                        pe.wait_ge(setup_act, ACT_DONE[before])
                    if before in DVE_DONE:
                        pe.wait_ge(setup_dve, DVE_DONE[before])

            def mm(dst, lhsT, rhs, start, stop):
                return nc.tensor.matmul(dst, lhsT, rhs, start=start, stop=stop)

            pe.wait_ge(ident_set, 1)
            pe.wait_ge(a1_in, 16)
            for k in range(KC):
                last = nc.tensor.transpose(bank_of("a1T")[:, PART * k:PART * k + PART],
                                           a1_sb[:, PART * k:PART * k + PART], ident[:, :])
            last.then_inc(setup_ps, 1)
            pe.wait_ge(w2_in, 16)
            for n in range(E2 // 2):
                last = nc.tensor.transpose(bank_of("w2T")[0:SEQ, PART * n:PART * n + PART],
                                           w2_sb[:, n, :], ident[:, :])
            last.then_inc(setup_ps, 1)
            pe.wait_ge(w1_in, 16)
            for k in range(KC):
                for o in range(KC):
                    last = nc.tensor.transpose(bank_of(f"g1_{k}")[:, PART * o:PART * o + PART],
                                               w1_sb[:, o, PART * k:PART * k + PART], ident[:, :])
                last.then_inc(setup_ps, 1)
            pe.wait_ge(a0_in, 16)
            for k in range(KC):
                last = nc.tensor.transpose(bank_of("a0T")[:, R0 * k:R0 * k + R0],
                                           a0_sb[:, PART * k:PART * k + PART], ident[0:R0, 0:R0])
            last.then_inc(setup_ps, 1)
            pe.wait_ge(wp_in, 16)
            for s in range(KC):
                free_bank(f"wpT_{s}")
                for o in range(KC):
                    src = wp_sb[:, o, s::KC]
                    last = nc.tensor.transpose(bank_of(f"wpT_{s}")[:, PART * o:PART * o + PART], src, ident[:, :])
                last.then_inc(setup_ps, 1)
            free_bank("v1")
            pe.wait_ge(b_scaled, 2)
            for s in range(KC):
                last = nc.tensor.transpose(bank_of("v1")[:, PART * s:PART * s + PART],
                                           b1_by[:, s, :, :].rearrange("p e r -> p (e r)"), ident[:, :])
            last.then_inc(setup_ps, 1)

            pe.wait_ge(wb_plus, KC)
            pe.wait_ge(setup_dve, DVE_DONE["g1_3"])
            pe.wait_ge(setup_act, ACT_DONE["g1_3"])
            for t in range(KC):
                free_bank(f"g01_{t}")
                for k in range(KC):
                    last = mm(bank_of(f"g01_{t}")[:, :], wb_sb[:, k, PART * t:PART * t + PART], g1[:, k, :],
                              k == 0, k == KC - 1)
                last.then_inc(setup_ps, 1)
            free_bank("gu1")
            for t in range(KC):
                for k in range(KC):
                    last = mm(bank_of("gu1")[:, PART * t:PART * t + PART], wb_sb[:, k, PART * t:PART * t + PART],
                              a1T[:, k, :], k == 0, k == KC - 1)
            last.then_inc(setup_ps, 1)
            pe.wait_ge(wt_in, 16)
            pe.wait_ge(setup_dve, DVE_DONE["a0T"])
            free_bank("u0")
            for t in range(KC):
                for k in range(KC):
                    last = mm(bank_of("u0")[:, R0 * t:R0 * t + R0], wt_sb[:, k, PART * t:PART * t + PART],
                              a0T[:, k, :], k == 0, k == KC - 1)
            last.then_inc(setup_ps, 1)
            free_bank("v0T")
            pe.wait_ge(setup_act, ACT_DONE["wpT_3"])
            for t in range(KC):
                for s in range(KC):
                    last = mm(bank_of("v0T")[:, R0 * t:R0 * t + R0], wpT[:, s, PART * t:PART * t + PART],
                              b0_by[:, s, :, :].rearrange("p e r -> p (e r)"), s == 0, s == KC - 1)
            last.then_inc(setup_ps, 1)
            pe.wait_ge(setup_dve, DVE_DONE["v0T"])
            free_bank("cross")
            for k in range(KC):
                last = mm(bank_of("cross")[:, 0:R0], a1T[:, k, :], v0T[:, k, 0, :], k == 0, k == KC - 1)
            last.then_inc(setup_ps, 1)
            free_bank("v0g1")
            for k in range(KC):
                last = mm(bank_of("v0g1")[:, :], v0T[:, k, :, :].rearrange("p t r -> p (t r)"), g1[:, k, :],
                          k == 0, k == KC - 1)
            last.then_inc(setup_ps, 1)
            pe.wait_ge(setup_dve, DVE_DONE["cross"])
            for n in range(E1 // 2):
                free_bank(f"t0_{n}")
                mm(bank_of(f"t0_{n}")[:, :], cross[:, 2 * n:2 * n + 2, :].rearrange("p f r -> p (f r)"), v1[:, :],
                   True, True).then_inc(setup_ps, 1)

            def token_mix(i):
                pe.wait_ge(w2_placed, 2 * QUAD * (i + 1))
                pe.wait_ge(w3_plus, i + 1)
                wait(pe, pl_set, 2 * i)
                for u in range(QUAD):
                    last = mm(p_ps[:, SEQ * u:SEQ * u + SEQ], w2_diag[u][:, :],
                              w3_all[:, bass.ds(QUAD * i + u, 1), :].rearrange("p a d -> p (a d)"), True, True)
                last.then_inc(p_done, 1)

            def mix(i, u):
                i, u = i + u // QUAD, u % QUAD
                pe.wait_ge(xl_set, QUAD * i + u + 1)
                wait(pe, yl_set, QUAD * i + u - 1)
                if u == 0:
                    pe.wait_ge(pl_set, 2 * (i + 1))
                p_high = ph[:, bass.ds(QUAD * i + u, 1), :].rearrange("p a d -> p (a d)")
                p_low = pl[:, bass.ds(QUAD * i + u, 1), :].rearrange("p a d -> p (a d)")
                for k in range(KC):
                    dst = y_ps[u % 2][:, PART * k:PART * k + PART]
                    cols = slice(PART * k, PART * k + PART)
                    mm(dst, xh[u % 2][:, cols], p_high, True, False)
                    mm(dst, xh[u % 2][:, cols], p_low, False, False)
                    last = mm(dst, xl[u % 2][:, cols], p_high, False, True)
                last.then_inc(y_done, 1)

            def step(i, u, last):
                if u == 1 and not last:
                    token_mix(i + 1)
                if not (last and u == QUAD - 1):
                    mix(i, u + 1)
                n = u % 2
                pe.wait_ge(yl_set, QUAD * i + u + 1)
                pe.wait_ge(u_placed, 4 * (QUAD * i + u + 1))
                wait(pe, zl_set, 2 * (QUAD * i + u - 1))
                z = z_ps[n][:, 0:PART]
                for k in range(KC):
                    mm(z, u_sel[n][:, 0, k, :], yh[n][:, k, :], k == 0, False)
                    mm(z, u_sel[n][:, 0, k, :], yl[n][:, k, :], False, False)
                    done = mm(z, u_sel[n][:, 1, k, :], yh[n][:, k, :], False, k == KC - 1)
                done.then_inc(z_done, 1)
                wait(pe, o_set, QUAD * i + u - 1)
                for k in range(KC):
                    mm(o_ps[n][:, :], yh[n][:, k, :], gh[:, k, :], k == 0, False)
                    mm(o_ps[n][:, :], yh[n][:, k, :], gl[:, k, :], False, False)
                    mm(o_ps[n][:, :], yl[n][:, k, :], gh[:, k, :], False, False)
                pe.wait_ge(zl_set, 2 * (QUAD * i + u + 1))
                pe.wait_ge(v_in[u], 64 * (i + 1))
                mm(o_ps[n][:, :], zh[n][:, :], v_sel[u][:, :], False, False)
                mm(o_ps[n][:, :], zl[n][:, :], v_sel[u][:, :], False, True).then_inc(o_done, 1)

            pe.wait_ge(setup_dve, DVE_DONE["t0_3"])
            pe.wait_ge(setup_act, ACT_DONE["v0g1"])
            token_mix(0)
            mix(0, 0)
            for u in range(QUAD):
                step(0, u, False)
            with pe.Fori(1, QUADS - 1) as i:
                for u in range(QUAD):
                    step(i, u, False)
            for u in range(QUAD):
                step(QUADS - 1, u, True)


_INS = ['x', 'itok_B_0_3', 'itok_B_0_6', 'itok_B_0_7', 'itok_B_1_198',
        'L0_cond_W_base', 'L0_cond_Wt', 'L0_cond_A', 'L0_cond_B_w', 'L0_cond_Wp', 'L0_cond_scaling',
        'L1_cond_W', 'L1_cond_A', 'L1_cond_Bm', 'L1_cond_scalings', 'L2_cond_weights', 'L3_cond_weights']


def kernel(**inputs):
    import numpy as _np
    import concourse.bacc as _bacc
    from concourse import mybir as _mybir
    from concourse.bass_utils import run_bass_kernel_spmd as _run

    nc = _bacc.Bacc("TRN2", target_bir_lowering=False, num_devices=1)
    arrays, args = {}, []
    for name in _INS:
        a = _np.ascontiguousarray(inputs[name])
        arrays[f"in_{name}_dram"] = a
        args.append(nc.dram_tensor(f"in_{name}_dram", a.shape, _mybir.dt.from_np(a.dtype), kind="ExternalInput").ap())
    args.append(nc.dram_tensor("out_dram", (BATCH, SEQ, D), F32, kind="ExternalOutput").ap())
    build(nc, *args)
    r = _run(nc, [arrays], core_ids=[0])
    return r.results[0]["out_dram"]
```

```python
from contextlib import ExitStack

import concourse.bass as bass
from concourse import mybir

ALU = mybir.AluOpType
ACT = mybir.ActivationFunctionType
F32 = mybir.dt.float32
F32R = mybir.dt.float32r
I32 = mybir.dt.int32

PART = 128
BATCH = 64
SEQ = 64
D = 512
RANK = 16
E0 = 4
E1 = 8
E2 = 8
E3 = 200

KC = D // PART
PAIRS = BATCH * SEQ // PART
QUAD = 4
QUADS = PAIRS // QUAD
R0 = E0 * RANK
R1 = E1 * RANK
T0_ROWS = E1 * R0
ZR = 4 * RANK


def p_slot(i):
    return QUAD * (i & 1)


def wait(eng, sem, value):
    if not isinstance(value, int) or value > 0:
        eng.wait_ge(sem, value)


def build(nc, x, e0_ids, e1_ids, e2_ids, e3_ids, w_base, w_t, a0, b0, w_p, s0, w1, a1, b1, s1, w2, w3, out):
    ctx = ExitStack()
    with ctx:
        def sb(name, shape, dt=F32):
            return ctx.enter_context(nc.sbuf_tensor(name, shape, dt))

        def sem(name):
            return ctx.enter_context(nc.semaphore(name))

        v_table = nc.dram_tensor("v_table", [T0_ROWS + R1, 2 * D], F32, kind="Internal").ap()

        ident = sb("ident", [PART, PART])
        ident2 = sb("ident2", [PART, SEQ])
        owner = sb("owner", [PART, E1])
        ids = sb("ids", [PART, 4, BATCH], I32)
        code_part = sb("code_part", [1, 3, BATCH], I32)
        ef_code = sb("ef_code", [1, PAIRS], I32)
        g_code = sb("g_code", [1, QUADS], I32)
        lane = sb("lane", [PART, PAIRS], I32)
        lane64 = sb("lane64", [PART, PAIRS], I32)
        w3_rows = sb("w3_rows", [PART, PAIRS], I32)


        wb_sb = sb("wb_sb", [PART, KC, D])
        wt_sb = sb("wt_sb", [PART, KC, D])
        wp_sb = sb("wp_sb", [PART, KC, D])
        w1_sb = sb("w1_sb", [PART, KC, D])
        a0_sb = sb("a0_sb", [R0, D])
        a1_sb = sb("a1_sb", [PART, D])
        b0_sb = sb("b0_sb", [PART, E0, KC, RANK])
        b1_sb = sb("b1_sb", [PART, E1, KC, RANK])
        s0_sb = sb("s0_sb", [PART, E0])
        s1_sb = sb("s1_sb", [PART, E1])
        w2_sb = sb("w2_sb", [PART, E2 // 2, SEQ])

        b0_by = sb("b0_by", [PART, KC, E0, RANK])
        b1_by = sb("b1_by", [PART, KC, E1, RANK])
        g1 = sb("g1", [PART, KC, D])
        wpT = sb("wpT", [PART, KC, D])
        a0T = sb("a0T", [PART, KC, R0])
        a1T = sb("a1T", [PART, KC, R1])
        v0T = sb("v0T", [PART, KC, 2, R0])
        v1 = sb("v1", [PART, D])
        v1_parts = sb("v1_parts", [PART, 2, D], F32R)
        cross = sb("cross", [PART, E1, R0])
        v0g1 = sb("v0g1", [PART, D])
        t0_sum = sb("t0_sum", [PART, 2, D])
        t0_parts = sb("t0_parts", [PART, E1 // 2, 2, D], F32R)
        gh = sb("gh", [PART, KC, D], F32R)
        gl = sb("gl", [PART, KC, D], F32R)
        u_tab = sb("u_tab", [PART, 2, KC, E0 + E1, RANK], F32R)
        w2T = sb("w2T", [PART, E2, SEQ])
        w3_all = sb("w3_all", [PART, PAIRS, SEQ])
        p_mix = sb("p_mix", [PART, 2 * QUAD, 2, PART], F32R)

        w2_diag = [sb(f"w2_diag{u}", [PART, PART]) for u in range(QUAD)]
        x_raw = sb("x_raw", [PART, QUAD, D])
        xh = [sb(f"xh{n}", [PART, D], F32R) for n in range(2)]
        xl = [sb(f"xl{n}", [PART, D], F32R) for n in range(2)]
        yh = [sb(f"yh{n}", [PART, KC, PART], F32R) for n in range(2)]
        yl = [sb(f"yl{n}", [PART, KC, PART], F32R) for n in range(2)]
        y_rest = [sb(f"y_rest{n}", [PART, D]) for n in range(2)]
        u_sel = [sb(f"u_sel{n}", [PART, 2, KC, ZR], F32R) for n in range(2)]
        zh = [sb(f"zh{n}", [PART, PART], F32R) for n in range(2)]
        zl = [sb(f"zl{n}", [PART, PART], F32R) for n in range(2)]
        v_sel = [sb(f"v_sel{u}", [PART, 2, D], F32R) for u in range(QUAD)]
        o_sb = sb("o_sb", [PART, QUAD, D])

        y_ps = [ctx.enter_context(nc.psum_tensor(f"y_ps{n}", [PART, 2 * D], F32)) for n in range(2)]
        o_ps = [ctx.enter_context(nc.psum_tensor(f"o_ps{n}", [PART, D], F32)) for n in range(2)]
        z_ps = ctx.enter_context(nc.psum_tensor("z_ps", [PART, D], F32))
        p_ps = ctx.enter_context(nc.psum_tensor("p_ps", [PART, D], F32))
        bank = [y_ps[0][:, 0:D], y_ps[0][:, D:], y_ps[1][:, 0:D], y_ps[1][:, D:],
                o_ps[0][:, :], o_ps[1][:, :], z_ps[:, :], p_ps[:, :]]

        ones_set = sem("ones_set")
        ident_set = sem("ident_set")
        ident2_set = sem("ident2_set")
        zero_set = sem("zero_set")
        ids_in = sem("ids_in")
        a1_in, w1_in, wb_in = sem("a1_in"), sem("w1_in"), sem("wb_in")
        a0_in, wt_in, wp_in = sem("a0_in"), sem("wt_in"), sem("wp_in")
        b0_in, b1_in, w2_in = sem("b0_in"), sem("b1_in"), sem("w2_in")
        w3_in = sem("w3_in")
        wb_plus = sem("wb_plus")
        b_scaled = sem("b_scaled")
        w3_plus = sem("w3_plus")
        setup_ps = sem("setup_ps")
        setup_act = sem("setup_act")
        setup_dve = sem("setup_dve")
        table_out = sem("table_out")
        iota_set, code_step, code_set, rows_set = sem("iota_set"), sem("code_step"), sem("code_set"), sem("rows_set")
        w2_placed = sem("w2_placed")
        p_done, ph_set, pl_set = sem("p_done"), sem("ph_set"), sem("pl_set")
        x_in = [sem(f"x_in{h}") for h in range(2)]
        xh_set, xl_set = sem("xh_set"), sem("xl_set")
        y_done, yh_set, yl_set = sem("y_done"), sem("yh_set"), sem("yl_set")
        rest_set = sem("rest_set")
        u_placed = sem("u_placed")
        z_done, zh_set, zl_set = sem("z_done"), sem("zh_set"), sem("zl_set")
        v_in = [sem(f"v_in{u}") for u in range(QUAD)]
        o_done, o_set = sem("o_done"), sem("o_set")
        o_out = [sem(f"o_out{h}") for h in range(2)]

        x_rows = x.rearrange("(n b) s d -> n (b s) d", b=2).rearrange("n p d -> p n d")
        out_rows = out.rearrange("(n b) s d -> n (b s) d", b=2).rearrange("n p d -> p n d")
        w3_flat = w3.rearrange("e c d -> (e c) d")

        ORDER = ["g1_0", "g1_1", "g1_2", "g1_3", "wpT_0", "wpT_1", "wpT_2", "wpT_3",
                 "a1T", "v1", "v0T", "cross", "v0g1", "t0_0", "t0_1", "t0_2", "t0_3",
                 "w2T", "a0T", "u0", "gu1", "g01_0", "g01_1", "g01_2", "g01_3"]
        ACT_STEPS = ["g1_0", "g1_1", "g1_2", "g1_3", "wpT_0", "wpT_1", "wpT_2", "wpT_3",
                     "a1T", "v1", "v1_high", "v0g1", "t0_0_high", "t0_1_high", "t0_2_high", "t0_3_high",
                     "u0", "gu1", "g01_0", "g01_1", "g01_2", "g01_3"]
        DVE_STEPS = ["g1_0", "g1_1", "g1_2", "g1_3", "v1_low", "v0T", "cross",
                     "t0_0", "t0_1", "t0_0_low", "t0_2", "t0_1_low", "t0_3", "t0_2_low", "t0_3_low",
                     "w2T_0", "w2T", "a0T", "u0", "gu1", "g01_0", "g01_1", "g01_2", "g01_3"]
        ACT_DONE = {name: n + 1 for n, name in enumerate(ACT_STEPS)}
        DVE_DONE = {name: n + 1 for n, name in enumerate(DVE_STEPS)}
        place = {name: n for n, name in enumerate(ORDER)}

        def bank_of(name):
            return bank[place[name] % 8]

        block = ctx.enter_context(nc.Block())

        @block.sync
        def _(sp):
            sp.dma_start(w1_sb[:, :, :], w1.rearrange("(c p) d -> p c d", p=PART)).then_inc(w1_in, 16)
            sp.dma_start(wp_sb[:, :, :], w_p.rearrange("(c p) d -> p c d", p=PART)).then_inc(wp_in, 16)
            sp.dma_start(wt_sb[:, :, :], w_t.rearrange("(c p) d -> p c d", p=PART)).then_inc(wt_in, 16)
            sp.dma_start(wb_sb[:, :, :], w_base.rearrange("(c p) d -> p c d", p=PART)).then_inc(wb_in, 16)

            def load(i, h):
                wait(sp, xl_set, QUAD * (i - 1) + 2 * h + 2)
                sp.dma_start(x_raw[:, 2 * h:2 * h + 2, :],
                             x_rows[:, bass.ds(QUAD * i + 2 * h, 2), :]).then_inc(x_in[h], 16)

            def store(i, h):
                sp.wait_ge(o_set, QUAD * i + 2 * h + 2)
                sp.dma_start(out_rows[:, bass.ds(QUAD * i + 2 * h, 2), :],
                             o_sb[:, 2 * h:2 * h + 2, :]).then_inc(o_out[h], 16)

            for h in range(2):
                load(0, h)

            sp.wait_ge(code_set, 1)

            def fetch_v(i, u):
                wait(sp, o_done, QUAD * (i - 1) + u + 1)
                code = sp.value_load(ef_code[0:1, bass.ds(QUAD * i + u, 1)], min_val=0, max_val=(E0 * E1) ** 2 - 1)
                for b in range(2):
                    ef = (code >> (5 * b)) & (E0 * E1 - 1)
                    f = (code >> (5 * b + 2)) & (E1 - 1)
                    for part, row in ((0, ef * RANK), (1, f * RANK + T0_ROWS)):
                        to = 32 * b + 16 * part
                        sp.dma_start(v_sel[u][to:to + RANK, :, :].rearrange("p h d -> p (h d)").bitcast(F32),
                                     v_table[bass.ds(row, RANK), :]).then_inc(v_in[u], 16)

            sp.wait_ge(setup_dve, DVE_DONE["v1_low"])
            sp.dma_start(v_table[T0_ROWS:, :],
                         v1_parts[:, :, :].rearrange("p h d -> p (h d)").bitcast(F32)).then_inc(table_out, 16)
            for n in range(E1 // 2):
                sp.wait_ge(setup_dve, DVE_DONE[f"t0_{n}_low"])
                sp.dma_start(v_table[PART * n:PART * n + PART, :],
                             t0_parts[:, n, :, :].rearrange("p h d -> p (h d)").bitcast(F32)).then_inc(table_out, 16)
            sp.wait_ge(table_out, 16 * (1 + E1 // 2))
            sp.wait_ge(zero_set, 13)
            for u in range(QUAD):
                fetch_v(0, u)

            def turn(i, last=False):
                for h in range(2):
                    if not last:
                        load(i + 1, h)
                    store(i, h)
                    if not last:
                        for u in range(2 * h, 2 * h + 2):
                            fetch_v(i + 1, u)

            turn(0)
            with sp.Fori(1, QUADS - 1) as i:
                turn(i)
            turn(QUADS - 1, last=True)
            for h in range(2):
                sp.wait_ge(o_out[h], 16 * QUADS)

        @block.gpsimd
        def _(pool):
            nc.gpsimd.iota(lane[:, :], pattern=[[0, PAIRS]], base=0, channel_multiplier=1).then_inc(iota_set, 1)
            nc.gpsimd.memset(ident[:, :], 0.0).then_inc(ones_set, 1)
            nc.gpsimd.memset(owner[:, :], 1.0).then_inc(ones_set, 1)
            pool.wait_ge(ones_set, 2)
            nc.gpsimd.affine_select(out=ident[:, :], in_=ident[:, :], compare_op=ALU.not_equal, fill=1.0,
                                    base=0, pattern=[[-1, PART]], channel_multiplier=1).then_inc(ident_set, 1)
            nc.gpsimd.affine_select(out=owner[:, :], in_=owner[:, :], compare_op=ALU.is_ge, fill=0.0,
                                    base=0, pattern=[[-RANK, E1]], channel_multiplier=1).then_inc(ones_set, 1)
            pool.wait_ge(ones_set, 3)
            nc.gpsimd.affine_select(out=owner[:, :], in_=owner[:, :], compare_op=ALU.is_ge, fill=0.0,
                                    base=RANK - 1, pattern=[[RANK, E1]], channel_multiplier=-1).then_inc(ident_set, 1)
            for t in w2_diag:
                nc.gpsimd.memset(t[:, :], 0.0).then_inc(zero_set, 1)
            for t in zh + zl:
                nc.gpsimd.memset(t[:, :].bitcast(F32), 0.0).then_inc(zero_set, 1)
            for t in v_sel:
                nc.gpsimd.memset(t[:, :, :].bitcast(F32), 0.0).then_inc(zero_set, 1)
            nc.gpsimd.memset(p_mix[:, :, :, :].bitcast(F32), 0.0).then_inc(zero_set, 1)

            pool.wait_ge(rows_set, 1)
            for j in range(PAIRS):
                pool.indirect_dma_start(
                    out=w3_all[:, j, :], out_offset=None, in_=w3_flat,
                    in_offset=bass.IndirectOffsetOnAxis(ap=w3_rows[:, j:j + 1], axis=0)).then_inc(w3_in, 16)
            def place_u(i, u):
                code = pool.value_load(ef_code[0:1, bass.ds(QUAD * i + u, 1)], min_val=0, max_val=(E0 * E1) ** 2 - 1)
                for b in range(2):
                    for part, e in ((0, (code >> (5 * b)) & (E0 - 1)), (1, ((code >> (5 * b + 2)) & (E1 - 1)) + E0)):
                        col = 32 * b + 16 * part
                        nc.gpsimd.tensor_copy(
                            u_sel[u % 2][:, :, :, col:col + RANK],
                            u_tab[:, :, :, bass.ds(e, 1), :].rearrange("p h k a r -> p h k (a r)")
                        ).then_inc(u_placed, 1)

            pool.wait_ge(code_set, 1)
            pool.wait_ge(setup_dve, DVE_DONE["gu1"])
            for u in range(2):
                place_u(0, u)
            def turn(i, last=False):
                for u in range(QUAD):
                    if not (last and u >= 2):
                        pool.wait_ge(z_done, QUAD * i + u + 1)
                        place_u(i + (u + 2) // QUAD, (u + 2) % QUAD)

            turn(0)
            with pool.Fori(1, QUADS - 1) as i:
                turn(i)
            turn(QUADS - 1, last=True)

        @block.scalar
        def _(act):
            for n, t in enumerate((e0_ids, e1_ids, e2_ids, e3_ids)):
                act.dma_start(ids[:, n, :], t.partition_broadcast(PART)).then_inc(ids_in, 16)
            act.dma_start(b0_sb[:, :, :, :], b0.rearrange("e (p s) r -> p e s r", s=KC)).then_inc(b0_in, 16)
            act.dma_start(s0_sb[:, :], s0.partition_broadcast(PART)).then_inc(b0_in, 16)
            act.dma_start(b1_sb[:, :, :, :], b1.rearrange("e (p s) r -> p e s r", s=KC)).then_inc(b1_in, 16)
            act.dma_start(s1_sb[:, :], s1.partition_broadcast(PART)).then_inc(b1_in, 16)
            act.dma_start(a1_sb[:, :], a1.rearrange("f r d -> (f r) d")).then_inc(a1_in, 16)
            act.dma_start(a0_sb[:, :], a0.rearrange("e r d -> (e r) d")).then_inc(a0_in, 16)
            act.dma_start(w2_sb[:, :, :], w2.rearrange("(n g) c d -> (g c) n d", g=2)).then_inc(w2_in, 16)

            def read(name, dst, src):
                act.wait_ge(setup_ps, place[name] + 1)
                nc.scalar.activation(dst, src, ACT.Copy).then_inc(setup_act, 1)

            for k in range(KC):
                read(f"g1_{k}", g1[:, k, :], bank_of(f"g1_{k}"))
            for k in range(KC):
                read(f"wpT_{k}", wpT[:, k, :], bank_of(f"wpT_{k}"))
            read("a1T", a1T[:, :, :].rearrange("p k r -> p (k r)"), bank_of("a1T"))
            read("v1", v1[:, :].rearrange("p (n s) -> p s n", s=KC),
                 bank_of("v1").rearrange("p (s n) -> p s n", s=KC))
            act.wait_ge(setup_act, ACT_DONE["v1"])
            nc.scalar.activation(v1_parts[:, 0, :], v1[:, :], ACT.Copy).then_inc(setup_act, 1)
            read("v0g1", v0g1[:, :], bank_of("v0g1"))
            for n in range(E1 // 2):
                act.wait_ge(setup_dve, DVE_DONE[f"t0_{n}"])
                nc.scalar.activation(t0_parts[:, n, 0, :], t0_sum[:, n % 2, :], ACT.Copy).then_inc(setup_act, 1)
            read("u0", u_tab[:, 0, :, 0:E0, :].rearrange("p k e r -> p k (e r)"),
                 bank_of("u0")[:, 0:KC * R0].rearrange("p (k r) -> p k r", k=KC))
            read("gu1", u_tab[:, 0, :, E0:, :].rearrange("p k e r -> p k (e r)"),
                 bank_of("gu1").rearrange("p (k r) -> p k r", k=KC))
            for k in range(KC):
                read(f"g01_{k}", gh[:, k, :], bank_of(f"g01_{k}"))

            def split_x(i, u):
                i, u = i + u // QUAD, u % QUAD
                act.wait_ge(x_in[u // 2], 16 * (i + 1))
                wait(act, y_done, QUAD * i + u - 1)
                nc.scalar.activation(xh[u % 2][:, :], x_raw[:, u, :], ACT.Copy).then_inc(xh_set, 1)

            def high_y(i, u):
                i, u = i + u // QUAD, u % QUAD
                act.wait_ge(y_done, QUAD * i + u + 1)
                wait(act, o_done, QUAD * i + u - 1)
                nc.scalar.activation(yh[u % 2][:, :, :],
                                     y_ps[u % 2][:, :].rearrange("p (k h t) -> p h k t", k=KC, h=2)[:, 0],
                                     ACT.Copy).then_inc(yh_set, 1)

            def high_p(i):
                act.wait_ge(p_done, i + 1)
                wait(act, y_done, QUAD * (i - 1))
                for b in range(2):
                    rows = slice(SEQ * b, SEQ * b + SEQ)
                    nc.scalar.activation(p_mix[rows, bass.ds(p_slot(i), QUAD), 0, rows],
                                         p_ps[rows, 0:QUAD * SEQ].rearrange("p (n d) -> p n d", d=SEQ),
                                         ACT.Copy).then_inc(ph_set, 1)

            def copy_out(i, u):
                act.wait_ge(o_done, QUAD * i + u + 1)
                wait(act, o_out[u // 2], 16 * i)
                nc.scalar.activation(o_sb[:, u, :], o_ps[u % 2][:, :], ACT.Copy).then_inc(o_set, 1)

            def step(i, u, last):
                high_y_due = not (last and u == QUAD - 1)
                if high_y_due:
                    high_y(i, u + 1)
                act.wait_ge(z_done, QUAD * i + u + 1)
                wait(act, o_done, QUAD * i + u - 1)
                for b in range(2):
                    rows, toks = slice(ZR // 2 * b, ZR // 2 * b + ZR // 2), slice(SEQ * b, SEQ * b + SEQ)
                    nc.scalar.activation(zh[u % 2][rows, toks], z_ps[rows, toks], ACT.Copy).then_inc(zh_set, 1)
                if not (last and u >= QUAD - 2):
                    split_x(i, u + 2)
                if u == 1 and not last:
                    high_p(i + 1)
                copy_out(i, u)

            act.wait_ge(zero_set, 13)
            high_p(0)
            split_x(0, 0)
            split_x(0, 1)
            high_y(0, 0)
            for u in range(QUAD):
                step(0, u, False)
            with act.Fori(1, QUADS - 1) as i:
                for u in range(QUAD):
                    step(i, u, False)
            for u in range(QUAD):
                step(QUADS - 1, u, True)


        @block.vector
        def _(dve):
            def link(ins):
                steps[0] += 1
                ins.then_inc(code_step, 1)
                dve.wait_ge(code_step, steps[0])

            steps = [0]
            dve.wait_ge(ids_in, 64)
            dve.wait_ge(iota_set, 1)
            for b in range(2):
                half = slice(SEQ * b, SEQ * b + SEQ)
                link(nc.vector.tensor_scalar(lane64[half, :], lane[half, :], float(-SEQ * b), None, ALU.add))
                last = nc.vector.scalar_tensor_tensor(
                    out=w3_rows[half, :], in0=ids[half, 3, :].rearrange("p (j b) -> p b j", b=2)[:, b],
                    scalar=float(SEQ), in1=lane64[half, :], op0=ALU.mult, op1=ALU.add)
                if b == 0:
                    link(last)
            last.then_inc(rows_set, 1)
            link(nc.vector.scalar_tensor_tensor(out=code_part[:, 0, :], in0=ids[0:1, 1, :], scalar=float(E0),
                                                in1=ids[0:1, 0, :], op0=ALU.mult, op1=ALU.add))
            ef = code_part[:, 0, :].rearrange("p (j b) -> p b j", b=2)
            link(nc.vector.scalar_tensor_tensor(out=ef_code[:, :], in0=ef[:, 1], scalar=float(E0 * E1),
                                                in1=ef[:, 0], op0=ALU.mult, op1=ALU.add))
            src, n, step_of = ids[0:1, 2, :], BATCH // 2, float(E2)
            for to in (code_part[:, 1, 0:BATCH // 2], code_part[:, 2, 0:BATCH // 4], g_code[:, :]):
                two = src.rearrange("p (j b) -> p b j", b=2)
                last = nc.vector.scalar_tensor_tensor(out=to, in0=two[:, 1], scalar=step_of, in1=two[:, 0],
                                                      op0=ALU.mult, op1=ALU.add)
                src, step_of = to, step_of * step_of
                if to.shape[1] > QUADS:
                    link(last)
            last.then_inc(code_set, 1)

            dve.wait_ge(ident_set, 2)
            for b in range(2):
                half = slice(SEQ * b, SEQ * b + SEQ)
                nc.vector.tensor_copy(ident2[half, :], ident[half, half]).then_inc(ident2_set, 1)
            def read(name, dst, src, in1, op):
                dve.wait_ge(setup_ps, place[name] + 1)
                nc.vector.tensor_tensor(dst, src, in1, op).then_inc(setup_dve, 1)

            for k in range(KC):
                dve.wait_ge(setup_act, ACT_DONE[f"g1_{k}"])
                blk = slice(PART * k, PART * k + PART)
                read(f"g1_{k}", g1[:, k, blk], bank_of(f"g1_{k}")[:, blk], ident[:, :], ALU.add)
            for (b_in, b_sb, b_by, s_sb, n) in ((b0_in, b0_sb, b0_by, s0_sb, E0), (b1_in, b1_sb, b1_by, s1_sb, E1)):
                dve.wait_ge(b_in, 32)
                nc.vector.tensor_tensor(b_by[:, :, :, :].rearrange("p s e r -> p e s r"), b_sb[:, :, :, :],
                                        s_sb[:, :].unsqueeze(2).unsqueeze(3).to_broadcast([PART, n, KC, RANK]),
                                        ALU.mult).then_inc(b_scaled, 1)
            dve.wait_ge(setup_act, ACT_DONE["v1_high"])
            nc.vector.tensor_tensor(v1_parts[:, 1, :], v1[:, :], v1_parts[:, 0, :].bitcast(F32),
                                    ALU.subtract).then_inc(setup_dve, 1)
            dve.wait_ge(setup_ps, place["v0T"] + 1)
            nc.vector.tensor_copy(v0T[:, :, :, :],
                                  bank_of("v0T")[:, 0:KC * R0].rearrange("p (k r) -> p k r", k=KC).unsqueeze(2)
                                  .to_broadcast([PART, KC, 2, R0])).then_inc(setup_dve, 1)
            read("cross", cross[:, :, :], bank_of("cross")[:, 0:R0].unsqueeze(1).to_broadcast([PART, E1, R0]),
                 owner[:, :].unsqueeze(2).to_broadcast([PART, E1, R0]), ALU.mult)
            dve.wait_ge(wb_in, 16)
            for k in range(KC):
                blk = wb_sb[:, k, PART * k:PART * k + PART]
                nc.vector.tensor_tensor(blk, blk, ident[:, :], ALU.add).then_inc(wb_plus, 1)
            dve.wait_ge(setup_act, ACT_DONE["v0g1"])

            def t0_low(n):
                dve.wait_ge(setup_act, ACT_DONE[f"t0_{n}_high"])
                nc.vector.tensor_tensor(t0_parts[:, n, 1, :], t0_sum[:, n % 2, :],
                                        t0_parts[:, n, 0, :].bitcast(F32), ALU.subtract).then_inc(setup_dve, 1)

            for n in range(E1 // 2):
                if n >= 2:
                    dve.wait_ge(setup_dve, DVE_DONE[f"t0_{n - 2}_low"])
                read(f"t0_{n}", t0_sum[:, n % 2, :], bank_of(f"t0_{n}"), v0g1[:, :], ALU.add)
                if n > 0:
                    t0_low(n - 1)
            t0_low(E1 // 2 - 1)
            w2_bank = bank_of("w2T")[0:SEQ, :].rearrange("p (g c) -> p g c", c=SEQ)
            eye = ident[0:SEQ, 0:SEQ].unsqueeze(1).to_broadcast([SEQ, E2, SEQ])
            for b in range(2):
                read("w2T", w2T[SEQ * b:SEQ * b + SEQ, :, :], w2_bank, eye, ALU.add)
            dve.wait_ge(setup_ps, place["a0T"] + 1)
            nc.vector.tensor_copy(a0T[:, :, :].rearrange("p k r -> p (k r)"),
                                  bank_of("a0T")[:, 0:KC * R0]).then_inc(setup_dve, 1)
            dve.wait_ge(setup_act, ACT_DONE["u0"])
            read("u0", u_tab[:, 1, :, 0:E0, :].rearrange("p k e r -> p k (e r)"),
                 bank_of("u0")[:, 0:KC * R0].rearrange("p (k r) -> p k r", k=KC),
                 u_tab[:, 0, :, 0:E0, :].rearrange("p k e r -> p k (e r)").bitcast(F32), ALU.subtract)
            dve.wait_ge(setup_act, ACT_DONE["gu1"])
            read("gu1", u_tab[:, 1, :, E0:, :].rearrange("p k e r -> p k (e r)"),
                 bank_of("gu1").rearrange("p (k r) -> p k r", k=KC),
                 u_tab[:, 0, :, E0:, :].rearrange("p k e r -> p k (e r)").bitcast(F32), ALU.subtract)
            for k in range(KC):
                dve.wait_ge(setup_act, ACT_DONE[f"g01_{k}"])
                read(f"g01_{k}", gl[:, k, :], bank_of(f"g01_{k}"), gh[:, k, :].bitcast(F32), ALU.subtract)

            def split_x(i, u):
                i, u = i + u // QUAD, u % QUAD
                dve.wait_ge(xh_set, QUAD * i + u + 1)
                wait(dve, y_done, QUAD * i + u - 1)
                nc.vector.tensor_tensor(xl[u % 2][:, :], x_raw[:, u, :], xh[u % 2][:, :].bitcast(F32),
                                        ALU.subtract).then_inc(xl_set, 1)

            def low_y(i, u):
                i, u = i + u // QUAD, u % QUAD
                dve.wait_ge(yh_set, QUAD * i + u + 1)
                wait(dve, o_done, QUAD * i + u - 1)
                y = y_ps[u % 2][:, :].rearrange("p (k h t) -> p h k t", k=KC, h=2)
                rest = y_rest[u % 2][:, :].rearrange("p (k t) -> p k t", k=KC)
                nc.vector.tensor_tensor(rest, y[:, 0], yh[u % 2][:, :, :].bitcast(F32),
                                        ALU.subtract).then_inc(rest_set, 1)
                dve.wait_ge(rest_set, QUAD * i + u + 1)
                nc.vector.tensor_tensor(yl[u % 2][:, :, :], y[:, 1], rest, ALU.add).then_inc(yl_set, 1)

            def low_p(i):
                dve.wait_ge(ph_set, 2 * (i + 1))
                wait(dve, y_done, QUAD * (i - 1))
                for b in range(2):
                    rows = slice(SEQ * b, SEQ * b + SEQ)
                    now = p_mix[rows, bass.ds(p_slot(i), QUAD), :, rows].rearrange("p n h d -> p h n d")
                    nc.vector.tensor_tensor(now[:, 1],
                                            p_ps[rows, 0:QUAD * SEQ].rearrange("p (n d) -> p n d", d=SEQ),
                                            now[:, 0].bitcast(F32), ALU.subtract).then_inc(pl_set, 1)

            def add_w3(i):
                if isinstance(i, int) and i == 0:
                    dve.wait_ge(w3_in, 16 * PAIRS)
                w = w3_all[:, bass.ds(QUAD * i, QUAD), :]
                nc.vector.tensor_tensor(w, w, ident2[:, :].unsqueeze(1).to_broadcast([PART, QUAD, SEQ]),
                                        ALU.add).then_inc(w3_plus, 1)

            def place_w2(i):
                wait(dve, p_done, i)
                code = dve.value_load(g_code[0:1, bass.ds(i, 1)], min_val=0, max_val=E2 ** (2 * QUAD) - 1)
                for u in range(QUAD):
                    for b in range(2):
                        g = (code >> (3 * (2 * u + b))) & (E2 - 1)
                        rows = slice(SEQ * b, SEQ * b + SEQ)
                        nc.vector.tensor_copy(w2_diag[u][rows, rows],
                                              w2T[rows, bass.ds(g, 1), :].rearrange("p a c -> p (a c)")
                                              ).then_inc(w2_placed, 1)

            def step(i, u, last):
                if u == 0 and not last:
                    add_w3(i + 1)
                    place_w2(i + 1)
                if not (last and u == QUAD - 1):
                    low_y(i, u + 1)
                dve.wait_ge(zh_set, 2 * (QUAD * i + u + 1))
                wait(dve, o_done, QUAD * i + u - 1)
                for b in range(2):
                    rows, toks = slice(ZR // 2 * b, ZR // 2 * b + ZR // 2), slice(SEQ * b, SEQ * b + SEQ)
                    nc.vector.tensor_tensor(zl[u % 2][rows, toks], z_ps[rows, toks],
                                            zh[u % 2][rows, toks].bitcast(F32), ALU.subtract).then_inc(zl_set, 1)
                if not (last and u >= QUAD - 2):
                    split_x(i, u + 2)
                if u == 1 and not last:
                    low_p(i + 1)

            dve.wait_ge(ident2_set, 2)
            add_w3(0)
            dve.wait_ge(zero_set, 13)
            place_w2(0)
            low_p(0)
            split_x(0, 0)
            split_x(0, 1)
            low_y(0, 0)
            for u in range(QUAD):
                step(0, u, False)
            with dve.Fori(1, QUADS - 1) as i:
                for u in range(QUAD):
                    step(i, u, False)
            for u in range(QUAD):
                step(QUADS - 1, u, True)

        @block.tensor
        def _(pe):
            def free_bank(name):
                n = place[name] - 8
                if n >= 0:
                    before = ORDER[n]
                    if before in ACT_DONE:
                        pe.wait_ge(setup_act, ACT_DONE[before])
                    if before in DVE_DONE:
                        pe.wait_ge(setup_dve, DVE_DONE[before])

            def mm(dst, lhsT, rhs, start, stop):
                return nc.tensor.matmul(dst, lhsT, rhs, start=start, stop=stop)

            pe.wait_ge(ident_set, 1)
            pe.wait_ge(w1_in, 16)
            for k in range(KC):
                for o in range(KC):
                    last = nc.tensor.transpose(bank_of(f"g1_{k}")[:, PART * o:PART * o + PART],
                                               w1_sb[:, o, PART * k:PART * k + PART], ident[:, :])
                last.then_inc(setup_ps, 1)
            pe.wait_ge(wp_in, 16)
            for s in range(KC):
                for o in range(KC):
                    last = nc.tensor.transpose(bank_of(f"wpT_{s}")[:, PART * o:PART * o + PART],
                                               wp_sb[:, o, s::KC], ident[:, :])
                last.then_inc(setup_ps, 1)
            pe.wait_ge(a1_in, 16)
            free_bank("a1T")
            for k in range(KC):
                last = nc.tensor.transpose(bank_of("a1T")[:, PART * k:PART * k + PART],
                                           a1_sb[:, PART * k:PART * k + PART], ident[:, :])
            last.then_inc(setup_ps, 1)
            free_bank("v1")
            pe.wait_ge(b_scaled, 2)
            for s in range(KC):
                last = nc.tensor.transpose(bank_of("v1")[:, PART * s:PART * s + PART],
                                           b1_by[:, s, :, :].rearrange("p e r -> p (e r)"), ident[:, :])
            last.then_inc(setup_ps, 1)
            free_bank("v0T")
            pe.wait_ge(setup_act, ACT_DONE["wpT_3"])
            for t in range(KC):
                for s in range(KC):
                    last = mm(bank_of("v0T")[:, R0 * t:R0 * t + R0], wpT[:, s, PART * t:PART * t + PART],
                              b0_by[:, s, :, :].rearrange("p e r -> p (e r)"), s == 0, s == KC - 1)
            last.then_inc(setup_ps, 1)
            pe.wait_ge(setup_dve, DVE_DONE["v0T"])
            pe.wait_ge(setup_act, ACT_DONE["a1T"])
            free_bank("cross")
            for k in range(KC):
                last = mm(bank_of("cross")[:, 0:R0], a1T[:, k, :], v0T[:, k, 0, :], k == 0, k == KC - 1)
            last.then_inc(setup_ps, 1)
            free_bank("v0g1")
            for k in range(KC):
                last = mm(bank_of("v0g1")[:, :], v0T[:, k, :, :].rearrange("p t r -> p (t r)"), g1[:, k, :],
                          k == 0, k == KC - 1)
            last.then_inc(setup_ps, 1)
            pe.wait_ge(setup_dve, DVE_DONE["cross"])
            pe.wait_ge(setup_act, ACT_DONE["v1"])
            for n in range(E1 // 2):
                free_bank(f"t0_{n}")
                mm(bank_of(f"t0_{n}")[:, :], cross[:, 2 * n:2 * n + 2, :].rearrange("p f r -> p (f r)"), v1[:, :],
                   True, True).then_inc(setup_ps, 1)
            pe.wait_ge(w2_in, 16)
            free_bank("w2T")
            for n in range(E2 // 2):
                last = nc.tensor.transpose(bank_of("w2T")[0:SEQ, PART * n:PART * n + PART],
                                           w2_sb[:, n, :], ident[:, :])
            last.then_inc(setup_ps, 1)
            pe.wait_ge(a0_in, 16)
            free_bank("a0T")
            for k in range(KC):
                last = nc.tensor.transpose(bank_of("a0T")[:, R0 * k:R0 * k + R0],
                                           a0_sb[:, PART * k:PART * k + PART], ident[0:R0, 0:R0])
            last.then_inc(setup_ps, 1)
            pe.wait_ge(wt_in, 16)
            pe.wait_ge(setup_dve, DVE_DONE["a0T"])
            free_bank("u0")
            for t in range(KC):
                for k in range(KC):
                    last = mm(bank_of("u0")[:, R0 * t:R0 * t + R0], wt_sb[:, k, PART * t:PART * t + PART],
                              a0T[:, k, :], k == 0, k == KC - 1)
            last.then_inc(setup_ps, 1)
            pe.wait_ge(wb_plus, KC)
            free_bank("gu1")
            for t in range(KC):
                for k in range(KC):
                    last = mm(bank_of("gu1")[:, PART * t:PART * t + PART], wb_sb[:, k, PART * t:PART * t + PART],
                              a1T[:, k, :], k == 0, k == KC - 1)
            last.then_inc(setup_ps, 1)
            for t in range(KC):
                free_bank(f"g01_{t}")
                for k in range(KC):
                    last = mm(bank_of(f"g01_{t}")[:, :], wb_sb[:, k, PART * t:PART * t + PART], g1[:, k, :],
                              k == 0, k == KC - 1)
                last.then_inc(setup_ps, 1)

            def token_mix(i):
                pe.wait_ge(w2_placed, 2 * QUAD * (i + 1))
                pe.wait_ge(w3_plus, i + 1)
                wait(pe, pl_set, 2 * i)
                for u in range(QUAD):
                    last = mm(p_ps[:, SEQ * u:SEQ * u + SEQ], w2_diag[u][:, :],
                              w3_all[:, bass.ds(QUAD * i + u, 1), :].rearrange("p a d -> p (a d)"), True, True)
                last.then_inc(p_done, 1)

            def mix(i, u):
                i, u = i + u // QUAD, u % QUAD
                pe.wait_ge(xl_set, QUAD * i + u + 1)
                wait(pe, yl_set, QUAD * i + u - 1)
                if u == 0:
                    pe.wait_ge(pl_set, 2 * (i + 1))
                both = p_mix[:, bass.ds(p_slot(i) + u, 1), :, :].rearrange("p a h d -> p (a h d)")
                for k in range(KC):
                    at = 2 * PART * k
                    cols = slice(PART * k, PART * k + PART)
                    mm(y_ps[u % 2][:, at:at + 2 * PART], xh[u % 2][:, cols], both, True, False)
                    last = mm(y_ps[u % 2][:, at:at + PART], xl[u % 2][:, cols],
                              p_mix[:, bass.ds(p_slot(i) + u, 1), 0, :].rearrange("p a d -> p (a d)"), False, True)
                last.then_inc(y_done, 1)

            def step(i, u, last):
                if u == 1 and not last:
                    token_mix(i + 1)
                if not (last and u == QUAD - 1):
                    mix(i, u + 1)
                n = u % 2
                pe.wait_ge(yl_set, QUAD * i + u + 1)
                pe.wait_ge(u_placed, 4 * (QUAD * i + u + 1))
                wait(pe, zl_set, 2 * (QUAD * i + u))
                z = z_ps[0:ZR, 0:PART]
                for k in range(KC):
                    mm(z, u_sel[n][:, 0, k, :], yh[n][:, k, :], k == 0, False)
                    mm(z, u_sel[n][:, 0, k, :], yl[n][:, k, :], False, False)
                    done = mm(z, u_sel[n][:, 1, k, :], yh[n][:, k, :], False, k == KC - 1)
                done.then_inc(z_done, 1)
                wait(pe, o_set, QUAD * i + u - 1)
                for k in range(KC):
                    mm(o_ps[n][:, :], yh[n][:, k, :], gh[:, k, :], k == 0, False)
                    mm(o_ps[n][:, :], yh[n][:, k, :], gl[:, k, :], False, False)
                    mm(o_ps[n][:, :], yl[n][:, k, :], gh[:, k, :], False, False)
                pe.wait_ge(zl_set, 2 * (QUAD * i + u + 1))
                pe.wait_ge(v_in[u], 64 * (i + 1))
                mm(o_ps[n][:, :], zh[n][:, :], v_sel[u][:, 0, :], False, False)
                mm(o_ps[n][:, :], zh[n][:, :], v_sel[u][:, 1, :], False, False)
                mm(o_ps[n][:, :], zl[n][:, :], v_sel[u][:, 0, :], False, True).then_inc(o_done, 1)

            pe.wait_ge(setup_dve, DVE_DONE["g01_3"])
            token_mix(0)
            mix(0, 0)
            for u in range(QUAD):
                step(0, u, False)
            with pe.Fori(1, QUADS - 1) as i:
                for u in range(QUAD):
                    step(i, u, False)
            for u in range(QUAD):
                step(QUADS - 1, u, True)


_INS = ['x', 'itok_B_0_3', 'itok_B_0_6', 'itok_B_0_7', 'itok_B_1_198',
        'L0_cond_W_base', 'L0_cond_Wt', 'L0_cond_A', 'L0_cond_B_w', 'L0_cond_Wp', 'L0_cond_scaling',
        'L1_cond_W', 'L1_cond_A', 'L1_cond_Bm', 'L1_cond_scalings', 'L2_cond_weights', 'L3_cond_weights']


def kernel(**inputs):
    import numpy as _np
    import concourse.bacc as _bacc
    from concourse import mybir as _mybir
    from concourse.bass_utils import run_bass_kernel_spmd as _run

    nc = _bacc.Bacc("TRN2", target_bir_lowering=False, num_devices=1)
    arrays, args = {}, []
    for name in _INS:
        a = _np.ascontiguousarray(inputs[name])
        arrays[f"in_{name}_dram"] = a
        args.append(nc.dram_tensor(f"in_{name}_dram", a.shape, _mybir.dt.from_np(a.dtype), kind="ExternalInput").ap())
    args.append(nc.dram_tensor("out_dram", (BATCH, SEQ, D), F32, kind="ExternalOutput").ap())
    build(nc, *args)
    r = _run(nc, [arrays], core_ids=[0])
    return r.results[0]["out_dram"]
```

```python
from contextlib import ExitStack

import concourse.bass as bass
from concourse import mybir

ALU = mybir.AluOpType
ACT = mybir.ActivationFunctionType
F32 = mybir.dt.float32
F32R = mybir.dt.float32r
I32 = mybir.dt.int32

PART = 128
BATCH = 64
SEQ = 64
D = 512
RANK = 16
E0 = 4
E1 = 8
E2 = 8
E3 = 200

KC = D // PART
PAIRS = BATCH * SEQ // PART
QUAD = 4
QUADS = PAIRS // QUAD
EARLY_W3 = 25
R0 = E0 * RANK
R1 = E1 * RANK
T0_ROWS = E1 * R0
ZR = 4 * RANK


def p_slot(i):
    return QUAD * (i & 1)


def wait(eng, sem, value):
    if not isinstance(value, int) or value > 0:
        eng.wait_ge(sem, value)


def build(nc, x, e0_ids, e1_ids, e2_ids, e3_ids, w_base, w_t, a0, b0, w_p, s0, w1, a1, b1, s1, w2, w3, out):
    ctx = ExitStack()
    with ctx:
        def sb(name, shape, dt=F32, of=ctx):
            return of.enter_context(nc.sbuf_tensor(name, shape, dt))

        def sem(name):
            return ctx.enter_context(nc.semaphore(name))

        v_table = nc.dram_tensor("v_table", [T0_ROWS + R1, 2 * D], F32, kind="Internal").ap()

        ident = sb("ident", [PART, PART])
        ident2 = sb("ident2", [PART, SEQ])
        owner = sb("owner", [PART, E1])
        ids = sb("ids", [PART, 4, BATCH], I32)
        code_part = sb("code_part", [1, 3, BATCH], I32)
        ef_code = sb("ef_code", [1, PAIRS], I32)
        g_code = sb("g_code", [1, QUADS], I32)
        lane = sb("lane", [PART, PAIRS], I32)
        lane64 = sb("lane64", [PART, PAIRS], I32)
        w3_rows = sb("w3_rows", [PART, PAIRS], I32)


        first = ExitStack()
        w1_sb = sb("w1_sb", [PART, KC, D], of=first)
        wp_sb = sb("wp_sb", [PART, KC, D], of=first)
        first.close()
        g01 = sb("g01", [PART, 2, KC, D], F32R)

        second = ExitStack()
        wb_sb = sb("wb_sb", [PART, KC, D], of=second)
        wt_sb = sb("wt_sb", [PART, KC, D], of=second)
        second.close()
        xh = [sb(f"xh{n}", [PART, D], F32R) for n in range(2)]
        xl = [sb(f"xl{n}", [PART, D], F32R) for n in range(2)]
        y_rest = [sb(f"y_rest{n}", [PART, D]) for n in range(2)]
        u_sel = [sb(f"u_sel{n}", [PART, 2, KC, ZR], F32R) for n in range(2)]

        third = ExitStack()
        wpT = sb("wpT", [PART, 2, KC, D], F32R, of=third)
        third.close()
        t0_parts = sb("t0_parts", [PART, E1 // 2, 2, D], F32R, of=third)
        third.close()
        o_sb = sb("o_sb", [PART, QUAD, D])
        yh = [sb(f"yh{n}", [PART, KC, PART], F32R) for n in range(2)]
        yl = [sb(f"yl{n}", [PART, KC, PART], F32R) for n in range(2)]

        wt = sb("wt", [PART, 2, KC, D], F32R)
        wb = sb("wb", [PART, 2, KC, D], F32R)
        g1 = sb("g1", [PART, 2, KC, D], F32R)
        a0_sb = sb("a0_sb", [R0, D])
        a1_sb = sb("a1_sb", [PART, D])
        b0_sb = sb("b0_sb", [PART, E0, KC, RANK])
        b1_sb = sb("b1_sb", [PART, E1, KC, RANK])
        s0_sb = sb("s0_sb", [PART, E0])
        s1_sb = sb("s1_sb", [PART, E1])
        w2_sb = sb("w2_sb", [PART, E2 // 2, SEQ])
        b0_by = sb("b0_by", [PART, 2, KC, E0, RANK], F32R)
        b0_now = sb("b0_now", [PART, KC, E0, RANK])
        b1_by = sb("b1_by", [PART, KC, E1, RANK])
        a0T = sb("a0T", [PART, 2, KC, R0], F32R)
        a1T = sb("a1T", [PART, 2, KC, R1], F32R)
        v0 = sb("v0", [R0, D])
        v0T = sb("v0T", [PART, 2, KC, 2, R0], F32R)
        u0T = sb("u0T", [R0, D])
        gu1T = sb("gu1T", [PART, D])
        v1 = sb("v1", [PART, D])
        v1_parts = sb("v1_parts", [PART, 2, D], F32R)
        cross_all = sb("cross_all", [PART, E1, R0])
        cross = sb("cross", [PART, 2, E1, R0], F32R)
        v0g1 = sb("v0g1", [PART, D])
        t0_sum = sb("t0_sum", [PART, 2, D])
        u_tab = sb("u_tab", [PART, 2, KC, E0 + E1, RANK], F32R)
        w2T = sb("w2T", [PART, E2, SEQ])
        w3_all = sb("w3_all", [PART, PAIRS, SEQ])
        p_mix = sb("p_mix", [PART, 2 * QUAD, 2, PART], F32R)

        w2_diag = [sb(f"w2_diag{u}", [PART, PART]) for u in range(QUAD)]
        x_raw = sb("x_raw", [PART, QUAD, D])
        z = [sb(f"z{n}", [PART, PART], F32R) for n in range(2)]
        v_sel = [sb(f"v_sel{u}", [PART, 2, D], F32R) for u in range(QUAD)]

        y_ps = [ctx.enter_context(nc.psum_tensor(f"y_ps{n}", [PART, 2 * D], F32)) for n in range(2)]
        o_ps = [ctx.enter_context(nc.psum_tensor(f"o_ps{n}", [PART, D], F32)) for n in range(2)]
        z_ps = ctx.enter_context(nc.psum_tensor("z_ps", [PART, D], F32))
        p_ps = ctx.enter_context(nc.psum_tensor("p_ps", [PART, D], F32))
        bank = [y_ps[0][:, 0:D], y_ps[0][:, D:], y_ps[1][:, 0:D], y_ps[1][:, D:],
                o_ps[0][:, :], o_ps[1][:, :], z_ps[:, :], p_ps[:, :]]

        ones_set = sem("ones_set")
        ident_set = sem("ident_set")
        ident2_set = sem("ident2_set")
        zero_set = sem("zero_set")
        ids_in, e3_in = sem("ids_in"), sem("e3_in")
        a1_in, w1_in, wb_in = sem("a1_in"), sem("w1_in"), sem("wb_in")
        a0_in, wt_in = sem("a0_in"), sem("wt_in")
        wp_in = [sem(f"wp_in{h}") for h in range(2)]
        b0_in, b1_in, w2_in = sem("b0_in"), sem("b1_in"), sem("w2_in")
        w3_in = [sem(f"w3_in{n}") for n in range(3)]
        w1_plus, wb_plus = sem("w1_plus"), sem("wb_plus")
        b_scaled = sem("b_scaled")
        w3_plus = sem("w3_plus")
        setup_ps = sem("setup_ps")
        setup_act = sem("setup_act")
        setup_dve = sem("setup_dve")
        table_out = sem("table_out")
        iota_set, code_step, code_set, rows_set = sem("iota_set"), sem("code_step"), sem("code_set"), sem("rows_set")
        w2_placed = sem("w2_placed")
        p_done, ph_set, pl_set = sem("p_done"), sem("ph_set"), sem("pl_set")
        x_in = [sem(f"x_in{h}") for h in range(2)]
        xh_set, xl_set = sem("xh_set"), sem("xl_set")
        y_done, yh_set, yl_set = sem("y_done"), sem("yh_set"), sem("yl_set")
        rest_set = sem("rest_set")
        u_placed = sem("u_placed")
        z_done, zh_set, zl_set = sem("z_done"), sem("zh_set"), sem("zl_set")
        v_in = [sem(f"v_in{u}") for u in range(QUAD)]
        v_twice = sem("v_twice")
        o_done, o_set = sem("o_done"), sem("o_set")
        o_out = [sem(f"o_out{h}") for h in range(2)]

        x_rows = x.rearrange("(n b) s d -> n (b s) d", b=2).rearrange("n p d -> p n d")
        out_rows = out.rearrange("(n b) s d -> n (b s) d", b=2).rearrange("n p d -> p n d")
        w3_flat = w3.rearrange("e c d -> (e c) d")

        ORDER = {"wpT_0": 0, "wpT_1": 1, "wpT_2": 2, "wpT_3": 3, "v0": 4, "a1T": 1, "g1_0": 5, "v0T": 2,
                 "g1_1": 6, "g1_2": 7, "g1_3": 0, "cross": 3, "w2T": 2, "a0T": 4, "v1": 0, "v0g1": 6, "gu1T": 7,
                 "g01_0": 1, "t0_0": 2, "t0_1": 3, "t0_2": 4, "t0_3": 5, "gu1": 6, "u0T": 7,
                 "g01_1": 0, "u0": 1, "g01_2": 2, "g01_3": 3}
        ACT_STEPS = ["wpT_0", "b0_high", "wpT_1", "wpT_2", "wpT_3", "v0", "a1T", "g1_0", "v0T", "g1_1",
                     "g1_2", "g1_3", "wb_high_0", "wb_high_1", "a0T", "cross_high", "v1", "v1_high",
                     "wt_high", "v0g1", "gu1T", "g01_0", "t0_0_high", "t0_1_high", "t0_2_high", "t0_3_high",
                     "gu1", "u0T", "g01_1", "u0", "g01_2", "g01_3"]
        DVE_STEPS = ["wpT_0", "wpT_1", "wpT_2", "wpT_3", "b0_low", "a1T", "v0T", "g1_0", "g1_1",
                     "g1_2", "g1_3", "wb_low_0", "wb_low_1", "cross", "cross_low", "w2T_0", "w2T", "v1_low", "a0T",
                     "wt_low", "g01_0", "t0_0", "t0_1", "t0_0_low", "t0_2", "t0_1_low", "t0_3", "t0_2_low",
                     "t0_3_low", "gu1", "g01_1", "u0", "g01_2", "g01_3"]
        ACT_DONE = {name: n + 1 for n, name in enumerate(ACT_STEPS)}
        DVE_DONE = {name: n + 1 for n, name in enumerate(DVE_STEPS)}
        place = {name: n for n, name in enumerate(ORDER)}

        def bank_of(name):
            return bank[ORDER[name]]

        block = ctx.enter_context(nc.Block())

        @block.sync
        def _(sp):
            wp_rows = w_p.rearrange("(c p) d -> p c d", p=PART)
            sp.dma_start(wp_sb[:, 0:2, :], wp_rows[:, 0:2, :]).then_inc(wp_in[0], 16)
            sp.dma_start(ids[:, 3, :], e3_ids.partition_broadcast(PART)).then_inc(e3_in, 16)
            sp.dma_start(wp_sb[:, 2:4, :], wp_rows[:, 2:4, :]).then_inc(wp_in[1], 16)
            sp.dma_start(b0_sb[:, :, :, :], b0.rearrange("e (p s) r -> p e s r", s=KC)).then_inc(b0_in, 16)
            sp.dma_start(s0_sb[:, :], s0.partition_broadcast(PART)).then_inc(b0_in, 16)
            sp.dma_start(w1_sb[:, :, :], w1.rearrange("(c p) d -> p c d", p=PART)).then_inc(w1_in, 16)
            for n, t in enumerate((e0_ids, e1_ids, e2_ids)):
                sp.dma_start(ids[:, n, :], t.partition_broadcast(PART)).then_inc(ids_in, 16)
            sp.dma_start(a1_sb[:, :], a1.rearrange("f r d -> (f r) d")).then_inc(a1_in, 16)
            sp.dma_start(wb_sb[:, :, :], w_base.rearrange("(c p) d -> p c d", p=PART)).then_inc(wb_in, 16)
            sp.dma_start(b1_sb[:, :, :, :], b1.rearrange("e (p s) r -> p e s r", s=KC)).then_inc(b1_in, 16)
            sp.dma_start(s1_sb[:, :], s1.partition_broadcast(PART)).then_inc(b1_in, 16)
            sp.dma_start(a0_sb[:, :], a0.rearrange("e r d -> (e r) d")).then_inc(a0_in, 16)
            sp.dma_start(w2_sb[:, :, :], w2.rearrange("(n g) c d -> (g c) n d", g=2)).then_inc(w2_in, 16)
            sp.dma_start(wt_sb[:, :, :], w_t.rearrange("(c p) d -> p c d", p=PART)).then_inc(wt_in, 16)

            def load(i, h):
                wait(sp, xl_set, QUAD * (i - 1) + 2 * h + 2)
                sp.dma_start(x_raw[:, 2 * h:2 * h + 2, :],
                             x_rows[:, bass.ds(QUAD * i + 2 * h, 2), :]).then_inc(x_in[h], 16)

            def store_last(u):
                sp.wait_ge(o_set, QUAD * (QUADS - 1) + u + 1)
                sp.dma_start(out_rows[:, PAIRS - QUAD + u, :], o_sb[:, u, :]).then_inc(o_out[u // 2], 16)

            def store(i, h):
                sp.wait_ge(o_set, QUAD * i + 2 * h + 2)
                sp.dma_start(out_rows[:, bass.ds(QUAD * i + 2 * h, 2), :],
                             o_sb[:, 2 * h:2 * h + 2, :]).then_inc(o_out[h], 16)

            for h in range(2):
                load(0, h)

            def fetch_v(i, u):
                wait(sp, o_done, QUAD * (i - 1) + u + 1)
                code = sp.value_load(ef_code[0:1, bass.ds(QUAD * i + u, 1)], min_val=0, max_val=(E0 * E1) ** 2 - 1)
                for b in range(2):
                    ef = (code >> (5 * b)) & (E0 * E1 - 1)
                    f = (code >> (5 * b + 2)) & (E1 - 1)
                    for part, row in ((0, ef * RANK), (1, f * RANK + T0_ROWS)):
                        to = 32 * b + 16 * part
                        sp.dma_start(v_sel[u][to:to + RANK, :, :].rearrange("p h d -> p (h d)").bitcast(F32),
                                     v_table[bass.ds(row, RANK), :]).then_inc(v_in[u], 16)

            sp.wait_ge(setup_dve, DVE_DONE["v1_low"])
            sp.dma_start(v_table[T0_ROWS:, :],
                         v1_parts[:, :, :].rearrange("p h d -> p (h d)").bitcast(F32)).then_inc(table_out, 16)
            for n in range(E1 // 2):
                sp.wait_ge(setup_dve, DVE_DONE[f"t0_{n}_low"])
                sp.dma_start(v_table[PART * n:PART * n + PART, :],
                             t0_parts[:, n, :, :].rearrange("p h d -> p (h d)").bitcast(F32)).then_inc(table_out, 16)
            sp.wait_ge(table_out, 16 * (1 + E1 // 2))
            sp.wait_ge(zero_set, 7 + QUAD)
            sp.wait_ge(code_set, 1)
            for u in range(QUAD):
                fetch_v(0, u)

            def turn(i):
                for h in range(2):
                    load(i + 1, h)
                    store(i, h)
                    for u in range(2 * h, 2 * h + 2):
                        fetch_v(i + 1, u)

            turn(0)
            with sp.Fori(1, QUADS - 1) as i:
                turn(i)
            for u in range(QUAD):
                store_last(u)
            for h in range(2):
                sp.wait_ge(o_out[h], 16 * (QUADS - 1) + 32)

        @block.gpsimd
        def _(pool):
            nc.gpsimd.memset(ident[:, :], 0.0).then_inc(ones_set, 1)
            nc.gpsimd.iota(lane[:, :], pattern=[[0, PAIRS]], base=0, channel_multiplier=1).then_inc(iota_set, 1)
            nc.gpsimd.memset(owner[:, :], 1.0).then_inc(ones_set, 1)
            pool.wait_ge(ones_set, 2)
            nc.gpsimd.affine_select(out=ident[:, :], in_=ident[:, :], compare_op=ALU.not_equal, fill=1.0,
                                    base=0, pattern=[[-1, PART]], channel_multiplier=1).then_inc(ident_set, 1)
            nc.gpsimd.affine_select(out=owner[:, :], in_=owner[:, :], compare_op=ALU.is_ge, fill=0.0,
                                    base=0, pattern=[[-RANK, E1]], channel_multiplier=1).then_inc(ones_set, 1)
            pool.wait_ge(ones_set, 3)
            nc.gpsimd.affine_select(out=owner[:, :], in_=owner[:, :], compare_op=ALU.is_ge, fill=0.0,
                                    base=RANK - 1, pattern=[[RANK, E1]], channel_multiplier=-1).then_inc(ident_set, 1)
            for t in w2_diag:
                nc.gpsimd.memset(t[:, :], 0.0).then_inc(zero_set, 1)
            for t in z:
                nc.gpsimd.memset(t[:, :].bitcast(F32), 0.0).then_inc(zero_set, 1)
            nc.gpsimd.memset(p_mix[:, :, :, :].bitcast(F32), 0.0).then_inc(zero_set, 1)

            def gather_w3(pairs):
                for j in pairs:
                    pool.indirect_dma_start(
                        out=w3_all[:, j, :], out_offset=None, in_=w3_flat,
                        in_offset=bass.IndirectOffsetOnAxis(ap=w3_rows[:, j:j + 1], axis=0)
                    ).then_inc(w3_in[min(j // QUAD, 2)], 16)

            def place_u(i, u):
                code = pool.value_load(ef_code[0:1, bass.ds(QUAD * i + u, 1)], min_val=0, max_val=(E0 * E1) ** 2 - 1)
                for b in range(2):
                    for part, e in ((0, (code >> (5 * b)) & (E0 - 1)), (1, ((code >> (5 * b + 2)) & (E1 - 1)) + E0)):
                        col = 32 * b + 16 * part
                        nc.gpsimd.tensor_copy(
                            u_sel[u % 2][:, :, :, col:col + RANK],
                            u_tab[:, :, :, bass.ds(e, 1), :].rearrange("p h k a r -> p h k (a r)")
                        ).then_inc(u_placed, 1)

            pool.wait_ge(rows_set, 1)
            gather_w3(range(0, QUAD))
            pool.wait_ge(wb_in, 16)
            for k in range(KC):
                blk = wb_sb[:, k, PART * k:PART * k + PART]
                nc.gpsimd.tensor_tensor(blk, blk, ident[:, :], ALU.add).then_inc(wb_plus, 1)
            for t in v_sel:
                nc.gpsimd.memset(t[:, 1, :].bitcast(F32), 0.0).then_inc(zero_set, 1)
            gather_w3(range(QUAD, EARLY_W3))
            pool.wait_ge(code_set, 1)
            pool.wait_ge(setup_dve, DVE_DONE["u0"])
            for u in range(2):
                place_u(0, u)
            gather_w3(range(EARLY_W3, PAIRS))

            def turn(i, last=False):
                for u in range(QUAD):
                    if not (last and u >= 2):
                        pool.wait_ge(z_done, QUAD * i + u + 1)
                        place_u(i + (u + 2) // QUAD, (u + 2) % QUAD)

            turn(0)
            with pool.Fori(1, QUADS - 1) as i:
                turn(i)
            turn(QUADS - 1, last=True)

        @block.scalar
        def _(act):
            def read(name, dst, src):
                act.wait_ge(setup_ps, place[name] + 1)
                nc.scalar.activation(dst, src, ACT.Copy).then_inc(setup_act, 1)

            def read_table(name, first_e, heads, src):
                read(name, u_tab[:, 0, :, first_e:first_e + heads, :].rearrange("p k e r -> p k (e r)"),
                     src.rearrange("p (k r) -> p k r", k=KC))

            def high(dst, src):
                nc.scalar.activation(dst, src, ACT.Copy).then_inc(setup_act, 1)

            for s in range(KC):
                read(f"wpT_{s}", wpT[:, 0, s, :], bank_of(f"wpT_{s}"))
                if s == 0:
                    act.wait_ge(b_scaled, 1)
                    high(b0_by[:, 0, :, :, :], b0_now[:, :, :, :])
            read("v0", v0[:, :], bank_of("v0")[0:R0, :])
            read("a1T", a1T[:, 0, :, :].rearrange("p k r -> p (k r)"), bank_of("a1T"))
            for k in range(KC):
                read(f"g1_{k}", g1[:, 0, k, :], bank_of(f"g1_{k}"))
                if k == 0:
                    read("v0T", v0T[:, 0, :, :, :], bank_of("v0T")[:, 0:KC * R0].rearrange("p (k r) -> p k r", k=KC)
                         .unsqueeze(2).to_broadcast([PART, KC, 2, R0]))
            act.wait_ge(wb_plus, KC)
            for h in range(2):
                high(wb[:, 0, 2 * h:2 * h + 2, :], wb_sb[:, 2 * h:2 * h + 2, :])
            read("a0T", a0T[:, 0, :, :].rearrange("p k r -> p (k r)"), bank_of("a0T")[:, 0:KC * R0])
            act.wait_ge(setup_dve, DVE_DONE["cross"])
            high(cross[:, 0, :, :], cross_all[:, :, :])
            read("v1", v1[:, :].rearrange("p (n s) -> p s n", s=KC),
                 bank_of("v1").rearrange("p (s n) -> p s n", s=KC))
            act.wait_ge(setup_act, ACT_DONE["v1"])
            high(v1_parts[:, 0, :], v1[:, :])
            act.wait_ge(wt_in, 16)
            high(wt[:, 0, :, :], wt_sb[:, :, :])
            read("v0g1", v0g1[:, :], bank_of("v0g1"))
            read("gu1T", gu1T[:, :], bank_of("gu1T"))
            read("g01_0", g01[:, 0, 0, :], bank_of("g01_0"))
            for n in range(E1 // 2):
                act.wait_ge(setup_dve, DVE_DONE[f"t0_{n}"])
                high(t0_parts[:, n, 0, :], t0_sum[:, n % 2, :])
            read_table("gu1", E0, E1, bank_of("gu1"))
            read("u0T", u0T[:, :], bank_of("u0T")[0:R0, :])
            read("g01_1", g01[:, 0, 1, :], bank_of("g01_1"))
            read_table("u0", 0, E0, bank_of("u0")[:, 0:KC * R0])
            read("g01_2", g01[:, 0, 2, :], bank_of("g01_2"))

            def split_x(i, u):
                i, u = i + u // QUAD, u % QUAD
                act.wait_ge(x_in[u // 2], 16 * (i + 1))
                wait(act, y_done, QUAD * i + u - 1)
                nc.scalar.activation(xh[u % 2][:, :], x_raw[:, u, :], ACT.Copy).then_inc(xh_set, 1)

            def high_y(i, u):
                i, u = i + u // QUAD, u % QUAD
                act.wait_ge(y_done, QUAD * i + u + 1)
                wait(act, o_done, QUAD * i + u - 1)
                nc.scalar.activation(yh[u % 2][:, :, :],
                                     y_ps[u % 2][:, :].rearrange("p (k h t) -> p h k t", k=KC, h=2)[:, 0],
                                     ACT.Copy).then_inc(yh_set, 1)

            def high_p(i):
                act.wait_ge(p_done, i + 1)
                wait(act, y_done, QUAD * (i - 1))
                for b in range(2):
                    rows = slice(SEQ * b, SEQ * b + SEQ)
                    nc.scalar.activation(p_mix[rows, bass.ds(p_slot(i), QUAD), 0, rows],
                                         p_ps[rows, 0:QUAD * SEQ].rearrange("p (n d) -> p n d", d=SEQ),
                                         ACT.Copy).then_inc(ph_set, 1)

            def double_v(i, u):
                i, u = i + u // QUAD, u % QUAD
                act.wait_ge(v_in[u], 64 * (i + 1))
                wait(act, o_done, QUAD * (i - 1) + u + 1)
                nc.scalar.activation(v_sel[u][ZR:, 0, :], v_sel[u][0:ZR, 0, :].bitcast(F32),
                                     ACT.Copy).then_inc(v_twice, 1)

            def copy_out(i, u):
                act.wait_ge(o_done, QUAD * i + u + 1)
                wait(act, o_out[u // 2], 16 * i)
                nc.scalar.activation(o_sb[:, u, :], o_ps[u % 2][:, :], ACT.Copy).then_inc(o_set, 1)

            def step(i, u, last):
                high_y_due = not (last and u == QUAD - 1)
                if high_y_due:
                    high_y(i, u + 1)
                act.wait_ge(z_done, QUAD * i + u + 1)
                wait(act, o_done, QUAD * i + u - 1)
                for b in range(2):
                    rows, toks = slice(ZR // 2 * b, ZR // 2 * b + ZR // 2), slice(SEQ * b, SEQ * b + SEQ)
                    nc.scalar.activation(z[u % 2][rows, toks], z_ps[rows, toks], ACT.Copy).then_inc(zh_set, 1)
                if not (last and u >= QUAD - 2):
                    split_x(i, u + 2)
                if u == 1 and not last:
                    high_p(i + 1)
                if high_y_due:
                    double_v(i, u + 1)
                copy_out(i, u)

            act.wait_ge(zero_set, 7 + QUAD)
            act.wait_ge(setup_dve, DVE_DONE["wt_low"])
            high_p(0)
            split_x(0, 0)
            split_x(0, 1)
            read("g01_3", g01[:, 0, 3, :], bank_of("g01_3"))
            act.wait_ge(table_out, 16 * (1 + E1 // 2))
            high_y(0, 0)
            double_v(0, 0)
            for u in range(QUAD):
                step(0, u, False)
            with act.Fori(1, QUADS - 1) as i:
                for u in range(QUAD):
                    step(i, u, False)
            for u in range(QUAD):
                step(QUADS - 1, u, True)

        @block.vector
        def _(dve):
            def link(ins):
                steps[0] += 1
                ins.then_inc(code_step, 1)
                dve.wait_ge(code_step, steps[0])

            steps = [0]
            dve.wait_ge(e3_in, 16)
            dve.wait_ge(iota_set, 1)
            for b in range(2):
                half = slice(SEQ * b, SEQ * b + SEQ)
                link(nc.vector.tensor_scalar(lane64[half, :], lane[half, :], float(-SEQ * b), None, ALU.add))
                last = nc.vector.scalar_tensor_tensor(
                    out=w3_rows[half, :], in0=ids[half, 3, :].rearrange("p (j b) -> p b j", b=2)[:, b],
                    scalar=float(SEQ), in1=lane64[half, :], op0=ALU.mult, op1=ALU.add)
                if b == 0:
                    link(last)
            last.then_inc(rows_set, 1)

            def scale(n, b_in, b_sb, b_by, s_sb):
                dve.wait_ge(b_in, 32)
                nc.vector.tensor_tensor(b_by[:, :, :, :].rearrange("p s e r -> p e s r"), b_sb[:, :, :, :],
                                        s_sb[:, :].unsqueeze(2).unsqueeze(3).to_broadcast([PART, n, KC, RANK]),
                                        ALU.mult).then_inc(b_scaled, 1)

            def read(name, dst, src, in1, op):
                dve.wait_ge(setup_ps, place[name] + 1)
                nc.vector.tensor_tensor(dst, src, in1, op).then_inc(setup_dve, 1)

            def low(dst, src, high, ready):
                dve.wait_ge(setup_act, ACT_DONE[ready])
                nc.vector.tensor_tensor(dst, src, high.bitcast(F32), ALU.subtract).then_inc(setup_dve, 1)

            def read_low(name, dst, src, high):
                dve.wait_ge(setup_act, ACT_DONE[name])
                read(name, dst, src, high.bitcast(F32), ALU.subtract)

            def read_low_table(name, first_e, heads, src):
                now = u_tab[:, :, :, first_e:first_e + heads, :].rearrange("p h k e r -> p h k (e r)")
                read_low(name, now[:, 1], src.rearrange("p (k r) -> p k r", k=KC), now[:, 0])

            scale(E0, b0_in, b0_sb, b0_now, s0_sb)
            for s in range(KC):
                read_low(f"wpT_{s}", wpT[:, 1, s, :], bank_of(f"wpT_{s}"), wpT[:, 0, s, :])
            low(b0_by[:, 1, :, :, :], b0_now[:, :, :, :], b0_by[:, 0, :, :, :], "b0_high")
            dve.wait_ge(ident_set, 2)
            dve.wait_ge(w1_in, 16)
            for k in range(KC):
                blk = w1_sb[:, k, PART * k:PART * k + PART]
                nc.vector.tensor_tensor(blk, blk, ident[:, :], ALU.add).then_inc(w1_plus, 1)
            for b in range(2):
                half = slice(SEQ * b, SEQ * b + SEQ)
                nc.vector.tensor_copy(ident2[half, :], ident[half, half]).then_inc(ident2_set, 1)
            read_low("a1T", a1T[:, 1, :, :].rearrange("p k r -> p (k r)"), bank_of("a1T"),
                     a1T[:, 0, :, :].rearrange("p k r -> p (k r)"))
            read_low("v0T", v0T[:, 1, :, :, :], bank_of("v0T")[:, 0:KC * R0].rearrange("p (k r) -> p k r", k=KC)
                     .unsqueeze(2).to_broadcast([PART, KC, 2, R0]), v0T[:, 0, :, :, :])
            for k in range(KC):
                read_low(f"g1_{k}", g1[:, 1, k, :], bank_of(f"g1_{k}"), g1[:, 0, k, :])
            scale(E1, b1_in, b1_sb, b1_by, s1_sb)
            for h in range(2):
                low(wb[:, 1, 2 * h:2 * h + 2, :], wb_sb[:, 2 * h:2 * h + 2, :], wb[:, 0, 2 * h:2 * h + 2, :],
                    f"wb_high_{h}")
            read("cross", cross_all[:, :, :], bank_of("cross")[:, 0:R0].unsqueeze(1).to_broadcast([PART, E1, R0]),
                 owner[:, :].unsqueeze(2).to_broadcast([PART, E1, R0]), ALU.mult)
            low(cross[:, 1, :, :], cross_all[:, :, :], cross[:, 0, :, :], "cross_high")
            w2_bank = bank_of("w2T")[0:SEQ, :].rearrange("p (g c) -> p g c", c=SEQ)
            eye = ident[0:SEQ, 0:SEQ].unsqueeze(1).to_broadcast([SEQ, E2, SEQ])
            for b in range(2):
                read("w2T", w2T[SEQ * b:SEQ * b + SEQ, :, :], w2_bank, eye, ALU.add)
            low(v1_parts[:, 1, :], v1[:, :], v1_parts[:, 0, :], "v1_high")
            read_low("a0T", a0T[:, 1, :, :].rearrange("p k r -> p (k r)"), bank_of("a0T")[:, 0:KC * R0],
                     a0T[:, 0, :, :].rearrange("p k r -> p (k r)"))
            dve.wait_ge(ids_in, 48)
            link(nc.vector.scalar_tensor_tensor(out=code_part[:, 0, :], in0=ids[0:1, 1, :], scalar=float(E0),
                                                in1=ids[0:1, 0, :], op0=ALU.mult, op1=ALU.add))
            ef = code_part[:, 0, :].rearrange("p (j b) -> p b j", b=2)
            link(nc.vector.scalar_tensor_tensor(out=ef_code[:, :], in0=ef[:, 1], scalar=float(E0 * E1),
                                                in1=ef[:, 0], op0=ALU.mult, op1=ALU.add))
            src, step_of = ids[0:1, 2, :], float(E2)
            for to in (code_part[:, 1, 0:BATCH // 2], code_part[:, 2, 0:BATCH // 4], g_code[:, :]):
                two = src.rearrange("p (j b) -> p b j", b=2)
                last = nc.vector.scalar_tensor_tensor(out=to, in0=two[:, 1], scalar=step_of, in1=two[:, 0],
                                                      op0=ALU.mult, op1=ALU.add)
                src, step_of = to, step_of * step_of
                if to.shape[1] > QUADS:
                    link(last)
            last.then_inc(code_set, 1)

            low(wt[:, 1, :, :], wt_sb[:, :, :], wt[:, 0, :, :], "wt_high")
            read_low("g01_0", g01[:, 1, 0, :], bank_of("g01_0"), g01[:, 0, 0, :])
            for n in range(E1 // 2):
                if n >= 2:
                    dve.wait_ge(setup_dve, DVE_DONE[f"t0_{n - 2}_low"])
                read(f"t0_{n}", t0_sum[:, n % 2, :], bank_of(f"t0_{n}"), v0g1[:, :], ALU.add)
                if n > 0:
                    low(t0_parts[:, n - 1, 1, :], t0_sum[:, (n - 1) % 2, :], t0_parts[:, n - 1, 0, :],
                        f"t0_{n - 1}_high")
            low(t0_parts[:, n, 1, :], t0_sum[:, n % 2, :], t0_parts[:, n, 0, :], f"t0_{n}_high")

            def split_x(i, u):
                i, u = i + u // QUAD, u % QUAD
                dve.wait_ge(xh_set, QUAD * i + u + 1)
                wait(dve, y_done, QUAD * i + u - 1)
                nc.vector.tensor_tensor(xl[u % 2][:, :], x_raw[:, u, :], xh[u % 2][:, :].bitcast(F32),
                                        ALU.subtract).then_inc(xl_set, 1)

            def low_y(i, u):
                i, u = i + u // QUAD, u % QUAD
                dve.wait_ge(yh_set, QUAD * i + u + 1)
                wait(dve, o_done, QUAD * i + u - 1)
                y = y_ps[u % 2][:, :].rearrange("p (k h t) -> p h k t", k=KC, h=2)
                rest = y_rest[u % 2][:, :].rearrange("p (k t) -> p k t", k=KC)
                nc.vector.tensor_tensor(rest, y[:, 0], yh[u % 2][:, :, :].bitcast(F32),
                                        ALU.subtract).then_inc(rest_set, 1)
                dve.wait_ge(rest_set, QUAD * i + u + 1)
                nc.vector.tensor_tensor(yl[u % 2][:, :, :], y[:, 1], rest, ALU.add).then_inc(yl_set, 1)

            def low_p(i):
                dve.wait_ge(ph_set, 2 * (i + 1))
                wait(dve, y_done, QUAD * (i - 1))
                for b in range(2):
                    rows = slice(SEQ * b, SEQ * b + SEQ)
                    now = p_mix[rows, bass.ds(p_slot(i), QUAD), :, rows].rearrange("p n h d -> p h n d")
                    nc.vector.tensor_tensor(now[:, 1],
                                            p_ps[rows, 0:QUAD * SEQ].rearrange("p (n d) -> p n d", d=SEQ),
                                            now[:, 0].bitcast(F32), ALU.subtract).then_inc(pl_set, 1)

            def add_w3(i):
                if isinstance(i, int) and i < 2:
                    dve.wait_ge(w3_in[i], 16 * QUAD)
                else:
                    dve.wait_ge(w3_in[2], 16 * (PAIRS - 2 * QUAD))
                w = w3_all[:, bass.ds(QUAD * i, QUAD), :]
                nc.vector.tensor_tensor(w, w, ident2[:, :].unsqueeze(1).to_broadcast([PART, QUAD, SEQ]),
                                        ALU.add).then_inc(w3_plus, 1)

            def load_g(i):
                return dve.value_load(g_code[0:1, bass.ds(i, 1)], min_val=0, max_val=E2 ** (2 * QUAD) - 1)

            def place_w2(i, code, pairs):
                wait(dve, p_done, i)
                for u in pairs:
                    for b in range(2):
                        g = (code >> (3 * (2 * u + b))) & (E2 - 1)
                        rows = slice(SEQ * b, SEQ * b + SEQ)
                        nc.vector.tensor_copy(w2_diag[u][rows, rows],
                                              w2T[rows, bass.ds(g, 1), :].rearrange("p a c -> p (a c)")
                                              ).then_inc(w2_placed, 1)

            def turn(i, last=False):
                if not last:
                    add_w3(i + 1)
                    code = load_g(i + 1)
                for u in range(QUAD):
                    if not last and u < 2:
                        place_w2(i + 1, code, range(2 * u, 2 * u + 2))
                    if not (last and u == QUAD - 1):
                        low_y(i, u + 1)
                    dve.wait_ge(zh_set, 2 * (QUAD * i + u + 1))
                    for b in range(2):
                        rows, toks = slice(ZR // 2 * b, ZR // 2 * b + ZR // 2), slice(SEQ * b, SEQ * b + SEQ)
                        nc.vector.tensor_tensor(z[u % 2][ZR + ZR // 2 * b:ZR + ZR // 2 * (b + 1), toks], z_ps[rows, toks],
                                                z[u % 2][rows, toks].bitcast(F32), ALU.subtract).then_inc(zl_set, 1)
                    if not (last and u >= QUAD - 2):
                        split_x(i, u + 2)
                    if u == 1 and not last:
                        low_p(i + 1)

            dve.wait_ge(ident2_set, 2)
            add_w3(0)
            dve.wait_ge(zero_set, 7)
            dve.wait_ge(setup_dve, DVE_DONE["w2T"])
            dve.wait_ge(code_set, 1)
            place_w2(0, load_g(0), range(QUAD))
            read_low_table("gu1", E0, E1, bank_of("gu1"))
            read_low("g01_1", g01[:, 1, 1, :], bank_of("g01_1"), g01[:, 0, 1, :])
            read_low_table("u0", 0, E0, bank_of("u0")[:, 0:KC * R0])
            read_low("g01_2", g01[:, 1, 2, :], bank_of("g01_2"), g01[:, 0, 2, :])
            low_p(0)
            split_x(0, 0)
            split_x(0, 1)
            read_low("g01_3", g01[:, 1, 3, :], bank_of("g01_3"), g01[:, 0, 3, :])
            low_y(0, 0)
            turn(0)
            with dve.Fori(1, QUADS - 1) as i:
                turn(i)
            turn(QUADS - 1, last=True)

        @block.tensor
        def _(pe):
            def free_bank(name):
                last = None
                for before in list(ORDER)[:place[name]]:
                    if ORDER[before] == ORDER[name]:
                        last = before
                if last in ACT_DONE:
                    pe.wait_ge(setup_act, ACT_DONE[last])
                if last in DVE_DONE:
                    pe.wait_ge(setup_dve, DVE_DONE[last])

            def mm(dst, lhsT, rhs, start, stop):
                return nc.tensor.matmul(dst, lhsT, rhs, start=start, stop=stop)

            def product(dst, lhsT, rhs, chunks=KC):
                for k in range(chunks):
                    for a, b in ((0, 0), (0, 1), (1, 0)):
                        last = mm(dst, lhsT(a, k), rhs(b, k), k == 0 and a == b == 0, k == chunks - 1 and a == 1)
                return last

            def flip(name, src, chunks, rows=PART):
                for k in range(chunks):
                    last = nc.tensor.transpose(bank_of(name)[:, rows * k:rows * k + rows],
                                               src[:, PART * k:PART * k + PART], ident[0:rows, 0:rows])
                last.then_inc(setup_ps, 1)

            def g01_rows(t):
                free_bank(f"g01_{t}")
                product(bank_of(f"g01_{t}"), lambda a, k: wb[:, a, k, PART * t:PART * t + PART],
                        lambda b, k: g1[:, b, k, :]).then_inc(setup_ps, 1)

            def keep_warm(count):
                for _ in range(count):
                    nc.tensor.transpose(p_ps[:, 0:PART], ident[:, :], ident[:, :])

            pe.wait_ge(ident_set, 1)
            keep_warm(12)
            for h in range(2):
                pe.wait_ge(wp_in[h], 16)
                for s in range(KC):
                    for o in range(2 * h, 2 * h + 2):
                        last = nc.tensor.transpose(bank_of(f"wpT_{s}")[:, PART * o:PART * o + PART],
                                                   wp_sb[:, o, s::KC], ident[:, :])
                    if h == 1:
                        last.then_inc(setup_ps, 1)
            keep_warm(24)
            pe.wait_ge(setup_dve, DVE_DONE["b0_low"])
            product(bank_of("v0")[0:R0, :], lambda a, s: b0_by[:, a, s, :, :].rearrange("p e r -> p (e r)"),
                    lambda b, s: wpT[:, b, s, :]).then_inc(setup_ps, 1)
            pe.wait_ge(a1_in, 16)
            free_bank("a1T")
            flip("a1T", a1_sb, KC)
            pe.wait_ge(w1_plus, KC)
            for k in range(KC):
                free_bank(f"g1_{k}")
                for o in range(KC):
                    last = nc.tensor.transpose(bank_of(f"g1_{k}")[:, PART * o:PART * o + PART],
                                               w1_sb[:, o, PART * k:PART * k + PART], ident[:, :])
                last.then_inc(setup_ps, 1)
                if k == 0:
                    free_bank("v0T")
                    pe.wait_ge(setup_act, ACT_DONE["v0"])
                    flip("v0T", v0, KC, R0)
            free_bank("cross")
            pe.wait_ge(setup_dve, DVE_DONE["v0T"])
            product(bank_of("cross")[:, 0:R0], lambda a, k: a1T[:, a, k, :],
                    lambda b, k: v0T[:, b, k, 0, :]).then_inc(setup_ps, 1)
            pe.wait_ge(w2_in, 16)
            free_bank("w2T")
            for n in range(E2 // 2):
                last = nc.tensor.transpose(bank_of("w2T")[0:SEQ, PART * n:PART * n + PART],
                                           w2_sb[:, n, :], ident[:, :])
            last.then_inc(setup_ps, 1)
            pe.wait_ge(a0_in, 16)
            free_bank("a0T")
            flip("a0T", a0_sb, KC, R0)
            free_bank("v1")
            pe.wait_ge(b_scaled, 2)
            for s in range(KC):
                last = nc.tensor.transpose(bank_of("v1")[:, PART * s:PART * s + PART],
                                           b1_by[:, s, :, :].rearrange("p e r -> p (e r)"), ident[:, :])
            last.then_inc(setup_ps, 1)
            free_bank("v0g1")
            pe.wait_ge(setup_dve, DVE_DONE["g1_3"])
            product(bank_of("v0g1"), lambda a, k: v0T[:, a, k, :, :].rearrange("p t r -> p (t r)"),
                    lambda b, k: g1[:, b, k, :]).then_inc(setup_ps, 1)
            free_bank("gu1T")
            pe.wait_ge(setup_dve, DVE_DONE["wb_low_1"])
            product(bank_of("gu1T"), lambda a, k: a1T[:, a, k, :], lambda b, k: wb[:, b, k, :]).then_inc(setup_ps, 1)
            g01_rows(0)
            pe.wait_ge(setup_dve, DVE_DONE["v1_low"])
            for n in range(E1 // 2):
                free_bank(f"t0_{n}")
                product(bank_of(f"t0_{n}"), lambda a, k: cross[:, a, 2 * n:2 * n + 2, :].rearrange("p f r -> p (f r)"),
                        lambda b, k: v1_parts[:, b, :], chunks=1).then_inc(setup_ps, 1)
            free_bank("gu1")
            pe.wait_ge(setup_act, ACT_DONE["gu1T"])
            flip("gu1", gu1T, KC)
            free_bank("u0T")
            pe.wait_ge(setup_dve, DVE_DONE["wt_low"])
            product(bank_of("u0T")[0:R0, :], lambda a, k: a0T[:, a, k, :],
                    lambda b, k: wt[:, b, k, :]).then_inc(setup_ps, 1)
            g01_rows(1)
            free_bank("u0")
            pe.wait_ge(setup_act, ACT_DONE["u0T"])
            flip("u0", u0T, KC, R0)
            g01_rows(2)

            def token_mix(i):
                pe.wait_ge(w2_placed, 2 * QUAD * (i + 1))
                pe.wait_ge(w3_plus, i + 1)
                wait(pe, pl_set, 2 * i)
                for u in range(QUAD):
                    last = mm(p_ps[:, SEQ * u:SEQ * u + SEQ], w2_diag[u][:, :],
                              w3_all[:, bass.ds(QUAD * i + u, 1), :].rearrange("p a d -> p (a d)"), True, True)
                last.then_inc(p_done, 1)

            def mix(i, u):
                i, u = i + u // QUAD, u % QUAD
                pe.wait_ge(xl_set, QUAD * i + u + 1)
                wait(pe, yl_set, QUAD * i + u - 1)
                if u == 0:
                    pe.wait_ge(pl_set, 2 * (i + 1))
                both = p_mix[:, bass.ds(p_slot(i) + u, 1), :, :].rearrange("p a h d -> p (a h d)")
                for k in range(KC):
                    at = 2 * PART * k
                    cols = slice(PART * k, PART * k + PART)
                    mm(y_ps[u % 2][:, at:at + 2 * PART], xh[u % 2][:, cols], both, True, False)
                    last = mm(y_ps[u % 2][:, at:at + PART], xl[u % 2][:, cols],
                              p_mix[:, bass.ds(p_slot(i) + u, 1), 0, :].rearrange("p a d -> p (a d)"), False, True)
                last.then_inc(y_done, 1)

            def step(i, u, last):
                if not (last and u == QUAD - 1):
                    mix(i, u + 1)
                n = u % 2
                pe.wait_ge(yl_set, QUAD * i + u + 1)
                pe.wait_ge(u_placed, 4 * (QUAD * i + u + 1))
                wait(pe, zl_set, 2 * (QUAD * i + u))
                zt = z_ps[0:ZR, 0:PART]
                for k in range(KC):
                    mm(zt, u_sel[n][:, 0, k, :], yh[n][:, k, :], k == 0, False)
                    mm(zt, u_sel[n][:, 0, k, :], yl[n][:, k, :], False, False)
                    done = mm(zt, u_sel[n][:, 1, k, :], yh[n][:, k, :], False, k == KC - 1)
                done.then_inc(z_done, 1)
                if u == 1 and not last:
                    token_mix(i + 1)
                wait(pe, o_set, QUAD * i + u - 1)
                for k in range(KC):
                    mm(o_ps[n][:, :], yh[n][:, k, :], g01[:, 0, k, :], k == 0, False)
                    mm(o_ps[n][:, :], yh[n][:, k, :], g01[:, 1, k, :], False, False)
                    mm(o_ps[n][:, :], yl[n][:, k, :], g01[:, 0, k, :], False, False)
                pe.wait_ge(zl_set, 2 * (QUAD * i + u + 1))
                pe.wait_ge(v_twice, QUAD * i + u + 1)
                mm(o_ps[n][:, :], z[n][:, :], v_sel[u][:, 0, :], False, False)
                mm(o_ps[n][:, :], z[n][:, :], v_sel[u][:, 1, :], False, True).then_inc(o_done, 1)

            pe.wait_ge(setup_act, ACT_DONE["u0T"])
            token_mix(0)
            g01_rows(3)
            pe.wait_ge(setup_dve, DVE_DONE["u0"])
            mix(0, 0)
            pe.wait_ge(setup_dve, DVE_DONE["g01_3"])
            for u in range(QUAD):
                step(0, u, False)
            with pe.Fori(1, QUADS - 1) as i:
                for u in range(QUAD):
                    step(i, u, False)
            for u in range(QUAD):
                step(QUADS - 1, u, True)


_INS = ['x', 'itok_B_0_3', 'itok_B_0_6', 'itok_B_0_7', 'itok_B_1_198',
        'L0_cond_W_base', 'L0_cond_Wt', 'L0_cond_A', 'L0_cond_B_w', 'L0_cond_Wp', 'L0_cond_scaling',
        'L1_cond_W', 'L1_cond_A', 'L1_cond_Bm', 'L1_cond_scalings', 'L2_cond_weights', 'L3_cond_weights']


def kernel(**inputs):
    import numpy as _np
    import concourse.bacc as _bacc
    from concourse import mybir as _mybir
    from concourse.bass_utils import run_bass_kernel_spmd as _run

    nc = _bacc.Bacc("TRN2", target_bir_lowering=False, num_devices=1)
    arrays, args = {}, []
    for name in _INS:
        a = _np.ascontiguousarray(inputs[name])
        arrays[f"in_{name}_dram"] = a
        args.append(nc.dram_tensor(f"in_{name}_dram", a.shape, _mybir.dt.from_np(a.dtype), kind="ExternalInput").ap())
    args.append(nc.dram_tensor("out_dram", (BATCH, SEQ, D), F32, kind="ExternalOutput").ap())
    build(nc, *args)
    r = _run(nc, [arrays], core_ids=[0])
    return r.results[0]["out_dram"]
```
